# Optimizing a Trainium2 kernel written in Bass

```python
import numpy as np
import jax
import jax.numpy as jnp

def _softmax(x, axis=-1):
    return jax.nn.softmax(x, axis=axis)

def _gelu(x):
    return jax.nn.gelu(x, approximate=True)

def _silu(x):
    return jax.nn.silu(x)

def _sigmoid(x):
    return jax.nn.sigmoid(x)

def _layernorm(x, axis=-1, eps=1e-05):
    m = jnp.mean(x, axis=axis, keepdims=True)
    v = jnp.var(x, axis=axis, keepdims=True)
    return (x - m) / jnp.sqrt(v + eps)

def _scatter_add(tgt, idx, src, axis=0):
    return tgt.at[idx].add(src)

def _segment_sum(src, seg, n):
    return jax.ops.segment_sum(src, seg, n)
kernel_name = 'mk_flamingo_gated_d2_seqx_r4_c2dc47'

def setup_inputs(seed: int=0):
    np.random.seed(seed)
    _w = jnp.asarray

    def _rec_inputs():
        import jax
        import jax.numpy as jnp
        _rk = jax.random.key(seed)
        x = -0.0002928 + 1 * jax.random.normal(jax.random.fold_in(_rk, 1), (8, 512, 256), jnp.float32)
        _lenS = 512 - jax.random.randint(jax.random.fold_in(_rk, 7), (8,), 0, max(1, 512 // 4) + 1, jnp.int32)
        _lenS2 = 512 - jax.random.randint(jax.random.fold_in(_rk, 8), (8,), 0, max(1, 512 // 4) + 1, jnp.int32)
        _ctx_1024P = jax.random.normal(jax.random.fold_in(_rk, 11), (8, 16, 256), jnp.float32)
        _ctx_1024c = jax.random.dirichlet(jax.random.fold_in(_rk, 511), 0.3 * jnp.ones((16,), jnp.float32), (8, 512))
        _ctx_1024t = jnp.einsum('bsk,bkd->bsd', _ctx_1024c, _ctx_1024P)
        _ctx_1024t = _ctx_1024t * jax.lax.rsqrt(jnp.mean(jnp.square(_ctx_1024t)) + 1e-12) * 0.953939
        ctx_1024 = -1.39393e-06 + 0.999914 * (_ctx_1024t + 0.3 * jax.random.normal(jax.random.fold_in(_rk, 611), (8, 512, 256), jnp.float32))
        _g = jax.random.normal(jax.random.fold_in(_rk, 9001), (2, 2), jnp.float32)
        _g = jnp.sign(_g) * jnp.maximum(jnp.abs(_g), 1.0) + (_g == 0) * 1.0
        g_xattn = _g[0]
        g_ffn = _g[1]
        return (x, ctx_1024, g_xattn, g_ffn)
    x, ctx_1024, g_xattn, g_ffn = _rec_inputs()

    def _L0_xattn_setup():
        import jax, jax.numpy as jnp
        import numpy as np
        B, S, H, NH = (2, 512, 256, 4)
        DH = H // NH
        EPS_BACKEND = 1e-06
        EPS_LN = 1e-06

        def _mlstm_parallel_stabilized(q, k, v, igate_preact, fgate_preact):
            b, nh, s, dh = q.shape
            log_fg = jax.nn.log_sigmoid(fgate_preact)
            cs = jnp.concatenate([jnp.zeros((b, nh, 1), q.dtype), jnp.cumsum(log_fg[..., 0], axis=2)], axis=2)
            fg_matrix = cs[:, :, :, None] - cs[:, :, None, :]
            fg_matrix = fg_matrix[:, :, 1:, 1:]
            causal = jnp.tril(jnp.ones((s, s), dtype=bool))
            log_fg_matrix = jnp.where(causal, fg_matrix, -jnp.inf)
            log_D = log_fg_matrix + jnp.swapaxes(igate_preact, -2, -1)
            max_log_D = jnp.max(log_D, axis=-1, keepdims=True)
            D = jnp.exp(log_D - max_log_D)
            qk = jnp.einsum('bhsd,bhtd->bhst', q, k) / jnp.sqrt(jnp.asarray(dh, q.dtype))
            C = qk * D
            normalizer = jnp.maximum(jnp.abs(jnp.sum(C, axis=-1, keepdims=True)), jnp.exp(-max_log_D))
            C_norm = C / (normalizer + EPS_BACKEND)
            return jnp.einsum('bhst,bhtd->bhsd', C_norm, v)

        def _multihead_layernorm(x, scale):
            mean = jnp.mean(x, axis=-1, keepdims=True)
            var = jnp.var(x, axis=-1, keepdims=True)
            xn = (x - mean) * jax.lax.rsqrt(var + EPS_LN)
            return xn * scale.reshape(NH, 1, DH)
        key = jax.random.key(seed)
        kq, kk, kv, kib = jax.random.split(key, 4)
        q = jax.random.normal(kq, (B, S, H), dtype=jnp.float32)
        k = jax.random.normal(kk, (B, S, H), dtype=jnp.float32)
        v = jax.random.normal(kv, (B, S, H), dtype=jnp.float32)
        igate_kernel = jnp.zeros((3 * H, NH), dtype=jnp.float32)
        igate_bias = 0.1 * jax.random.normal(kib, (NH,), dtype=jnp.float32)
        fgate_kernel = jnp.zeros((3 * H, NH), dtype=jnp.float32)
        fgate_bias = jnp.linspace(3.0, 6.0, NH, dtype=jnp.float32)
        outnorm_scale = jnp.ones((H,), dtype=jnp.float32)
        return {'q': q, 'k': k, 'v': v, 'igate_kernel': igate_kernel, 'igate_bias': igate_bias, 'fgate_kernel': fgate_kernel, 'fgate_bias': fgate_bias, 'outnorm_scale': outnorm_scale}
    _L0_xattn_all = _L0_xattn_setup()
    _L0_xattn_in = {k: v for k, v in _L0_xattn_all.items() if k in ('igate_kernel', 'igate_bias', 'fgate_kernel', 'fgate_bias', 'outnorm_scale')}
    del _L0_xattn_all

    def _L0_ffn_setup():
        import jax, jax.numpy as jnp
        import numpy as np
        QB = 127.0
        EPS = 1e-05

        def _ste(x, q):
            return x + jax.lax.stop_gradient(q - x)

        def bitlinear(x, W, b):
            w_scale = jnp.clip(jnp.mean(jnp.abs(W)), EPS, None)
            Wq = _ste(W, jnp.clip(jnp.round(W / w_scale), -1.0, 1.0) * w_scale)
            x_scale = jnp.clip(jnp.max(jnp.abs(x), axis=-1, keepdims=True), EPS, None)
            xq = _ste(x, jnp.clip(jnp.round(x * (QB / x_scale)), -QB - 1.0, QB) * (x_scale / QB))
            return jnp.einsum('bnd,hd->bnh', xq, Wq) + b
        key = jax.random.key(seed)
        k0, k1, k2 = jax.random.split(key, 3)
        B, N, D = (8, 1024, 256)
        H = int(D * 4.0)
        x = jax.random.normal(k0, (B, N, D), dtype=jnp.float32)
        W1 = jax.random.normal(k1, (H, D), dtype=jnp.float32) * 0.02
        b1 = jnp.zeros((H,), dtype=jnp.float32)
        W2 = jax.random.normal(k2, (D, H), dtype=jnp.float32) * 0.02
        b2 = jnp.zeros((D,), dtype=jnp.float32)
        return {'x': x, 'W1': W1, 'b1': b1, 'W2': W2, 'b2': b2}
    _L0_ffn_all = _L0_ffn_setup()
    _L0_ffn_in = {k: v for k, v in _L0_ffn_all.items() if k in ('W1', 'b1', 'W2', 'b2')}
    del _L0_ffn_all

    def _L1_xattn_setup():
        import jax, jax.numpy as jnp
        import numpy as np
        HEADS = 16
        DIM_HEAD = 64
        SCALE = DIM_HEAD ** (-0.5)
        key = jax.random.key(seed)
        ks = jax.random.split(key, 5)
        B, S, D = (4, 512, 256)
        _dim = HEADS * DIM_HEAD
        return {'q': jax.random.normal(ks[0], (B, S, D), dtype=jnp.float32), 'kv': jax.random.normal(ks[1], (B, S, D), dtype=jnp.float32), 'Wq': jax.random.normal(ks[2], (_dim, D), dtype=jnp.float32) * 0.02, 'Wkv': jax.random.normal(ks[3], (2 * _dim, D), dtype=jnp.float32) * 0.02, 'W0': jax.random.normal(ks[4], (D, _dim), dtype=jnp.float32) * 0.02}
    _L1_xattn_all = _L1_xattn_setup()
    _L1_xattn_in = {k: v for k, v in _L1_xattn_all.items() if k in ('Wq', 'Wkv', 'W0')}
    del _L1_xattn_all

    def _L1_ffn_setup():
        import jax, jax.numpy as jnp
        import numpy as np
        D_MODEL, D_FF, N_EXPERTS, TOP_K = (256, 512, 8, 2)
        B, S = (2, 512)
        key = jax.random.key(seed)
        k1, k2, k3, k4 = jax.random.split(key, 4)
        scale = 0.02
        return {'x': jax.random.normal(k1, (B, S, D_MODEL), dtype=jnp.float32), 'gate_w': jax.random.normal(k2, (D_MODEL, N_EXPERTS), dtype=jnp.float32) * scale, 'w1': jax.random.normal(k3, (N_EXPERTS, D_MODEL, D_FF), dtype=jnp.float32) * scale, 'w2': jax.random.normal(k4, (N_EXPERTS, D_FF, D_MODEL), dtype=jnp.float32) * scale}
    _L1_ffn_all = _L1_ffn_setup()
    _L1_ffn_in = {k: v for k, v in _L1_ffn_all.items() if k in ('gate_w', 'w1', 'w2')}
    del _L1_ffn_all
    return {'x': x, 'ctx_1024': ctx_1024, 'g_xattn': g_xattn, 'g_ffn': g_ffn, 'L0_xattn_igate_kernel': _L0_xattn_in['igate_kernel'], 'L0_xattn_igate_bias': _L0_xattn_in['igate_bias'], 'L0_xattn_fgate_kernel': _L0_xattn_in['fgate_kernel'], 'L0_xattn_fgate_bias': _L0_xattn_in['fgate_bias'], 'L0_xattn_outnorm_scale': _L0_xattn_in['outnorm_scale'], 'L0_ffn_W1': _L0_ffn_in['W1'], 'L0_ffn_b1': _L0_ffn_in['b1'], 'L0_ffn_W2': _L0_ffn_in['W2'], 'L0_ffn_b2': _L0_ffn_in['b2'], 'L1_xattn_Wq': _L1_xattn_in['Wq'], 'L1_xattn_Wkv': _L1_xattn_in['Wkv'], 'L1_xattn_W0': _L1_xattn_in['W0'], 'L1_ffn_gate_w': _L1_ffn_in['gate_w'], 'L1_ffn_w1': _L1_ffn_in['w1'], 'L1_ffn_w2': _L1_ffn_in['w2']}

def reference(x, ctx_1024, g_xattn, g_ffn, L0_xattn_igate_kernel, L0_xattn_igate_bias, L0_xattn_fgate_kernel, L0_xattn_fgate_bias, L0_xattn_outnorm_scale, L0_ffn_W1, L0_ffn_b1, L0_ffn_W2, L0_ffn_b2, L1_xattn_Wq, L1_xattn_Wkv, L1_xattn_W0, L1_ffn_gate_w, L1_ffn_w1, L1_ffn_w2):
    import jax
    import jax.numpy as jnp

    def _L0_xattn_ref(q, k, v, igate_kernel, igate_bias, fgate_kernel, fgate_bias, outnorm_scale):
        import jax, jax.numpy as jnp
        import numpy as np
        B, S, H, NH = (2, 512, 256, 4)
        DH = H // NH
        EPS_BACKEND = 1e-06
        EPS_LN = 1e-06

        def _mlstm_parallel_stabilized(q, k, v, igate_preact, fgate_preact):
            b, nh, s, dh = q.shape
            log_fg = jax.nn.log_sigmoid(fgate_preact)
            cs = jnp.concatenate([jnp.zeros((b, nh, 1), q.dtype), jnp.cumsum(log_fg[..., 0], axis=2)], axis=2)
            fg_matrix = cs[:, :, :, None] - cs[:, :, None, :]
            fg_matrix = fg_matrix[:, :, 1:, 1:]
            causal = jnp.tril(jnp.ones((s, s), dtype=bool))
            log_fg_matrix = jnp.where(causal, fg_matrix, -jnp.inf)
            log_D = log_fg_matrix + jnp.swapaxes(igate_preact, -2, -1)
            max_log_D = jnp.max(log_D, axis=-1, keepdims=True)
            D = jnp.exp(log_D - max_log_D)
            qk = jnp.einsum('bhsd,bhtd->bhst', q, k) / jnp.sqrt(jnp.asarray(dh, q.dtype))
            C = qk * D
            normalizer = jnp.maximum(jnp.abs(jnp.sum(C, axis=-1, keepdims=True)), jnp.exp(-max_log_D))
            C_norm = C / (normalizer + EPS_BACKEND)
            return jnp.einsum('bhst,bhtd->bhsd', C_norm, v)

        def _multihead_layernorm(x, scale):
            mean = jnp.mean(x, axis=-1, keepdims=True)
            var = jnp.var(x, axis=-1, keepdims=True)
            xn = (x - mean) * jax.lax.rsqrt(var + EPS_LN)
            return xn * scale.reshape(NH, 1, DH)
        b, s, h = q.shape
        gate_in = jnp.concatenate([q, k, v], axis=-1)
        ig = gate_in @ igate_kernel + igate_bias
        fg = gate_in @ fgate_kernel + fgate_bias
        ig = jnp.transpose(ig, (0, 2, 1))[..., None]
        fg = jnp.transpose(fg, (0, 2, 1))[..., None]
        qh = jnp.transpose(q.reshape(b, s, NH, DH), (0, 2, 1, 3))
        kh = jnp.transpose(k.reshape(b, s, NH, DH), (0, 2, 1, 3))
        vh = jnp.transpose(v.reshape(b, s, NH, DH), (0, 2, 1, 3))
        hs = _mlstm_parallel_stabilized(qh, kh, vh, ig, fg)
        hn = _multihead_layernorm(hs, outnorm_scale)
        return jnp.transpose(hn, (0, 2, 1, 3)).reshape(b, s, h)

    def _L0_ffn_ref(x, W1, b1, W2, b2):
        import jax, jax.numpy as jnp
        import numpy as np
        QB = 127.0
        EPS = 1e-05

        def _ste(x, q):
            return x + jax.lax.stop_gradient(q - x)

        def bitlinear(x, W, b):
            w_scale = jnp.clip(jnp.mean(jnp.abs(W)), EPS, None)
            Wq = _ste(W, jnp.clip(jnp.round(W / w_scale), -1.0, 1.0) * w_scale)
            x_scale = jnp.clip(jnp.max(jnp.abs(x), axis=-1, keepdims=True), EPS, None)
            xq = _ste(x, jnp.clip(jnp.round(x * (QB / x_scale)), -QB - 1.0, QB) * (x_scale / QB))
            return jnp.einsum('bnd,hd->bnh', xq, Wq) + b
        h = bitlinear(x, W1, b1)
        h = jax.nn.gelu(h, approximate=False)
        return bitlinear(h, W2, b2)

    def _L1_xattn_ref(q, kv, Wq, Wkv, W0):
        import jax, jax.numpy as jnp
        import numpy as np
        HEADS = 16
        DIM_HEAD = 64
        SCALE = DIM_HEAD ** (-0.5)
        b, tq, _ = q.shape
        _, tk, _ = kv.shape
        qp = jnp.einsum('btm,em->bte', q, Wq)
        kvp = jnp.einsum('btm,em->bte', kv, Wkv)
        kvp = kvp.reshape(b, tk, DIM_HEAD, 2, HEADS)
        kvp = jnp.transpose(kvp, (3, 0, 4, 1, 2))
        k, v = (kvp[0], kvp[1])
        qh = jnp.transpose(qp.reshape(b, tq, DIM_HEAD, HEADS), (0, 3, 1, 2))
        scores = jnp.einsum('bhid,bhjd->bhij', qh, k) * SCALE
        attn = jax.nn.softmax(scores, axis=-1)
        attn = jnp.nan_to_num(attn)
        out = jnp.einsum('bhij,bhjd->bhid', attn, v)
        out = jnp.transpose(out, (0, 2, 1, 3)).reshape(b, tq, HEADS * DIM_HEAD)
        return jnp.einsum('bte,de->btd', out, W0)

    def _L1_ffn_ref(x, gate_w, w1, w2):
        import jax, jax.numpy as jnp
        import numpy as np
        D_MODEL, D_FF, N_EXPERTS, TOP_K = (256, 512, 8, 2)
        B, S = (2, 512)
        router_logits = jnp.einsum('bsd,de->bse', x, gate_w)
        top_logits, top_idx = jax.lax.top_k(router_logits, TOP_K)
        top_w = jax.nn.softmax(top_logits, axis=-1)
        combine = jnp.sum(jax.nn.one_hot(top_idx, N_EXPERTS, dtype=x.dtype) * top_w[..., None], axis=-2)
        h = jax.nn.silu(jnp.einsum('bsd,edf->ebsf', x, w1))
        y = jnp.einsum('ebsf,efd->ebsd', h, w2)
        out = jnp.einsum('ebsd,bse->bsd', y, combine)
        return out
    x = x + jnp.tanh(g_xattn[0]) * _L0_xattn_ref(_layernorm(x, axis=-1), ctx_1024, ctx_1024, L0_xattn_igate_kernel, L0_xattn_igate_bias, L0_xattn_fgate_kernel, L0_xattn_fgate_bias, L0_xattn_outnorm_scale)
    x = x + jnp.tanh(g_ffn[0]) * _L0_ffn_ref(_layernorm(x, axis=-1), L0_ffn_W1, L0_ffn_b1, L0_ffn_W2, L0_ffn_b2)
    x = x + jnp.tanh(g_xattn[1]) * _L1_xattn_ref(_layernorm(x, axis=-1), ctx_1024, L1_xattn_Wq, L1_xattn_Wkv, L1_xattn_W0)
    x = x + jnp.tanh(g_ffn[1]) * _L1_ffn_ref(_layernorm(x, axis=-1), L1_ffn_gate_w, L1_ffn_w1, L1_ffn_w2)
    return x

_drawn_inputs = setup_inputs


def setup_inputs(seed=0):
    import zlib

    import numpy as np

    out = dict(_drawn_inputs(seed))
    spreads = {'g_ffn': (-1.0, 0.6),
     'L0_xattn_igate_kernel': (0.0, 0.1),
     'L0_xattn_fgate_kernel': (0.0, 0.1),
     'L0_xattn_outnorm_scale': (1.0, 0.2),
     'L0_ffn_b1': (0.0, 0.617),
     'L0_ffn_b2': (0.0, 0.1)}
    factors = {'L0_xattn_igate_bias': 200.0, 'L1_xattn_Wq': 8.0}
    for name, (base, spread) in spreads.items():
        noise = np.random.default_rng([zlib.crc32(name.encode()), seed]).standard_normal(out[name].shape)
        drawn = base * np.exp(spread * noise) if base else spread * noise
        out[name] = jnp.asarray(drawn.astype(out[name].dtype))
    for name, factor in factors.items():
        out[name] = (out[name] * factor).astype(out[name].dtype)
    return out
```

```python
from contextlib import ExitStack

import concourse.bass as bass
from concourse import mybir

F32 = mybir.dt.float32
F32R = mybir.dt.float32r
BF16 = mybir.dt.bfloat16
U32 = mybir.dt.uint32
ALU = mybir.AluOpType
ACT = mybir.ActivationFunctionType
AX = mybir.AxisListType

P = 128
B, S, D = 8, 512, 256
NT = S // P
DC = D // P
TT = B * NT
H0, HD = 4, 64
F0 = 1024
H1 = 16
NE, FE = 8, 512
FC = FE // P
EPS_LN = 1e-5
EPS_HEAD = 1e-6
EPS_Q = 1e-5
QB = 127.0
ROUND = 12582912.0
LOWEST = -3.0e38
HUGE = 1.0e30


class Steps:

    def __init__(self, eng, sem, per=0):
        self.eng, self.sem, self.per, self.base, self.n = eng, sem, per, 0, 0

    def begin(self, it):
        self.base, self.n = it * self.per, 0

    def __call__(self, ins):
        ins.then_inc(self.sem, 1)
        self.n += 1
        self.eng.wait_ge(self.sem, self.base + self.n)

    def end(self):
        assert self.n == self.per, (self.n, self.per)


def stand_alone(eng, k):
    eng.sem_inc(k.passed, 1)


class Core:

    def __init__(self, nc, ctx):
        self.nc = nc
        self.passed = ctx.enter_context(nc.semaphore("waits_passed"))

        def sb(name, shape, dt=F32):
            return ctx.enter_context(nc.sbuf_tensor(name, shape, dt))

        self.x = sb("x_res", [P, TT, D])
        self.ctxT = sb("ctxT", [P, DC, B * S])
        self.xnT = sb("xnT", [P, DC, B * S])
        self.ident = sb("ident", [P, P])
        self.identb = sb("identb", [P, P], BF16)
        self.tg = sb("tanh_gates", [P, 4])
        self.neg_half = sb("neg_half", [P, 32])


def phase_scope(nc, tag):
    ctx = ExitStack()

    def sb(name, shape, dt=F32):
        return ctx.enter_context(nc.sbuf_tensor(f"{tag}_{name}", shape, dt))

    def ps(name, shape, dt=F32):
        return ctx.enter_context(nc.psum_tensor(f"{tag}_{name}", shape, dt))

    def sem(name):
        return ctx.enter_context(nc.semaphore(f"{tag}_{name}"))

    return ctx, sb, ps, sem


def load_phase(nc, k, d):
    ctx, sb, ps, sem = phase_scope(nc, "ld")
    with ctx:
        raw = sb("raw_gates", [P, 4])
        loaded, gates_in, blank, made = sem("loaded"), sem("gates_in"), sem("blank"), sem("made")
        with nc.Block() as block:
            @block.sync
            def _(sp):
                sp.dma_start(k.x[:], d["x"].rearrange("(t p) d -> p t d", p=P)).then_inc(loaded, 16)
                sp.dma_start(k.ctxT[:], d["ctxT"].rearrange("(c p) n -> p c n", p=P)).then_inc(loaded, 16)
                sp.wait_ge(loaded, 32)

            @block.scalar
            def _(act):
                for n, (g, at) in enumerate((("g_xattn", 0), ("g_ffn", 0), ("g_xattn", 1), ("g_ffn", 1))):
                    src = d[g][at:at + 1].rearrange("(a b) -> a b", a=1).broadcast_to([P, 1])
                    act.dma_start(raw[:, n:n + 1], src).then_inc(gates_in, 16)
                act.wait_ge(gates_in, 64)
                act.activation(k.tg[:], raw[:], ACT.Tanh).then_inc(made, 1)

            @block.gpsimd
            def _(pool):
                pool.memset(k.ident[:], 0.0).then_inc(blank, 1)
                pool.memset(k.identb[:], 0.0).then_inc(blank, 1)
                pool.memset(k.neg_half[:], -0.5).then_inc(blank, 1)
                pool.wait_ge(blank, 3)
                for m in (k.ident, k.identb):
                    pool.affine_select(out=m[:], in_=m[:], compare_op=ALU.not_equal, fill=1.0, base=0,
                                       pattern=[[-1, P]], channel_multiplier=1).then_inc(made, 1)


def norm_phase(nc, k, tag):
    ctx, sb, ps, sem = phase_scope(nc, tag)
    with ctx:
        stats = sb("stats", [P, 2, NT, 6])
        mv = sb("mean_var", [P, 2, NT, 2])
        veps = sb("var_eps", [P, 2, NT])
        rstd = sb("rstd", [P, 2, NT])
        xn = sb("xn", [P, 2, NT, D])
        tp = [ps(f"turned{i}", [P, S]) for i in range(2 * DC)]
        v_step, rstd_ready, xn_ready = sem("v_step"), sem("rstd_ready"), sem("xn_ready")
        turned, copied = sem("turned"), sem("copied")
        with nc.Block() as block:
            @block.vector
            def _(dve):
                step = Steps(dve, v_step, 3)
                with dve.Fori(0, B // 2) as i:
                    for u in range(2):
                        b = 2 * i + u
                        step.begin(b)
                        for t in range(NT):
                            last = dve.bn_stats(stats[:, u, t, :], k.x[:, bass.ds(NT * b + t, 1), :])
                        step(last)
                        stand_alone(dve, k)
                        for t in range(NT):
                            last = dve.bn_aggr(mv[:, u, t, :], stats[:, u, t, :])
                        step(last)
                        step(dve.tensor_scalar(veps[:, u, :], mv[:, u, :, 1], EPS_LN, None, ALU.add))
                        step.end()
                        dve.wait_ge(rstd_ready, b + 1)
                        dve.wait_ge(turned, b + 1)
                        for t in range(NT):
                            last = dve.tensor_scalar(xn[:, u, t, :], k.x[:, bass.ds(NT * b + t, 1), :],
                                                     mv[:, u, t, 0:1], rstd[:, u, t:t + 1],
                                                     ALU.subtract, ALU.mult)
                        last.then_inc(xn_ready, 1)

            @block.gpsimd
            def _(pool):
                with pool.Fori(0, B // 2) as i:
                    for u in range(2):
                        b = 2 * i + u
                        pool.wait_ge(v_step, 3 * b + 3)
                        pool.tensor_tensor(rstd[:, u, :], veps[:, u, :], k.neg_half[:, 0:NT],
                                           ALU.pow).then_inc(rstd_ready, 1)

            @block.scalar
            def _(act):
                act.sem_inc(copied, 2)
                with act.Fori(0, B // 2) as i:
                    for u in range(2):
                        b = 2 * i + u
                        act.wait_ge(turned, b + 3)
                        for c in range(DC):
                            last = act.activation(k.xnT[:, c, bass.ds(S * b, S)], tp[2 * u + c][:], ACT.Copy)
                        last.then_inc(copied, 1)

            @block.tensor
            def _(pe):
                pe.sem_inc(turned, 2)
                with pe.Fori(0, B // 2) as i:
                    for u in range(2):
                        b = 2 * i + u
                        pe.wait_ge(xn_ready, b + 1)
                        pe.wait_ge(copied, b + 1)
                        for c in range(DC):
                            for t in range(NT):
                                last = pe.transpose(tp[2 * u + c][:, t * P:(t + 1) * P],
                                                    xn[:, u, t, c * P:(c + 1) * P], k.ident[:])
                        last.then_inc(turned, 1)


GP = P + B - 1


def mlstm_phase(nc, k, d):
    ctx, sb, ps, sem = phase_scope(nc, "ml")
    R = 32 * H0
    with ctx:
        acol = sb("a_cols", [P, NT, H0, 32])
        exp_nmax = sb("exp_negmax_cols", [P, NT, H0, 32])
        m_rows = sb("M_rows", [P, B, S])
        scale_row = sb("scale_row", [P, D])
        with ExitStack() as gctx:
            _gates(nc, k, d, gctx, acol, exp_nmax, m_rows, scale_row)

        kz = sb("k_padded", [P, 2, DC, 2, S])
        va = sb("v_and_ones", [P, 2, NT, H0, HD + 1])
        mr = sb("M_rows_of_batch", [P, 2, S])
        mb = sb("M_all_partitions", [P, 2, S])
        md = sb("M_diagonal", [P, 2, NT, P])
        dt = sb("D_T", [P, 2, NT, S])
        oT = sb("o_T", [HD + 1, H0, S])
        o = sb("o", [P, 2, NT, H0, HD + 1])
        sq = sb("squares", [P, NT * H0, HD])
        st = sb("head_stats", [P, 8, NT * H0])
        y = sb("y", [P, 2, NT, D])
        qk = [ps(f"qk{j}", [P, S]) for j in range(NT)]
        op = ps("o_psum", [P, S])
        tp = [ps(f"o_turned{i}", [P, NT, HD + 1]) for i in range(2)]

        m_in = [sem("m_in0"), sem("m_in1")]
        zeroed, kv_in = sem("zeroed"), [sem("kv_in0"), sem("kv_in1")]
        qk_ready = sem("qk_ready")
        c_done = sem("c_done")
        cv_done = sem("cv_done")
        mb_ready = sem("mb_ready")
        d_exp = sem("d_exp")
        masked = sem("masked")
        ot_ready = sem("ot_ready")
        t_done = sem("t_done")
        o_ready = sem("o_ready")
        v_step, sq_ready, rs_ready = sem("v_step"), sem("sq_ready"), sem("rs_ready")
        y_ready = sem("y_ready")
        x_added = sem("x_added")
        p_step = sem("p_step")
        vsteps = 12
        with nc.Block() as block:
            @block.sync
            def _(sp):
                sp.wait_ge(zeroed, 2)
                with sp.Fori(0, B // 2) as i:
                    for u in range(2):
                        b = 2 * i + u
                        sp.wait_ge(cv_done, H0 * b + H0)
                        sp.wait_ge(mb_ready, H0 * b + H0)
                        for c in range(DC):
                            for half in range(2):
                                r = HD * half
                                sp.dma_start(kz[r:r + HD, u, c, half, :],
                                             d["ctxT"][c * P + r:c * P + r + HD, bass.ds(S * b, S)]).then_inc(kv_in[u], 16)
                        for h in range(H0):
                            r = 32 * h
                            sp.dma_start(mr[r:r + 1, u, :], m_rows[r:r + 1, bass.ds(b, 1), :].rearrange("p a s -> p (a s)")).then_inc(m_in[u], 16)
                        for j in range(NT):
                            src = d["ctx"][bass.ds(S * b + P * j, P), :].rearrange("p (h e) -> p h e", h=H0)
                            sp.dma_start(va[:, u, j, :, 0:HD], src).then_inc(kv_in[u], 16)

            @block.tensor
            def _(pe):
                pe.sem_inc(cv_done, 2 * H0)
                with pe.Fori(0, B // 2) as i:
                    for u in range(2):
                        b = 2 * i + u
                        pe.wait_ge(kv_in[u], 16 * 8 * (i + 1))

                        def turn(h):
                            n = H0 * b + h
                            pe.wait_ge(ot_ready, n + 2)
                            pe.wait_ge(o_ready, n + 1)
                            for j in range(NT):
                                last = pe.transpose(tp[h % 2][:, j, :], oT[:, h, j * P:(j + 1) * P],
                                                    k.ident[0:HD + 1, 0:HD + 1])
                            last.then_inc(t_done, 1)

                        for h in range(H0):
                            n = H0 * b + h
                            for j in range(NT):
                                w = S - P * j
                                pe.matmul(qk[j][:, 0:w], kz[:, u, h // 2, h % 2, j * P:(j + 1) * P],
                                          k.xnT[:, h // 2, bass.ds(S * b + P * j, w)],
                                          start=True, stop=True).then_inc(qk_ready, 1)
                            if h > 0:
                                turn(h - 1)
                            pe.wait_ge(ot_ready, n + 1)
                            for j in range(NT):
                                w = S - P * j
                                pe.wait_ge(c_done, NT * n + j + 1)
                                last = pe.matmul(op[0:HD + 1, j * P:S], va[:, u, j, h, :],
                                                 dt[:, h % 2, j, 0:w], start=(j == 0), stop=(j == NT - 1))
                            last.then_inc(cv_done, 1)
                        turn(H0 - 1)

            @block.gpsimd
            def _(pool):
                pool.sem_inc(x_added, 2)
                pool.sem_inc(masked, 1)
                pool.sem_inc(mb_ready, 2 * H0)
                huge = pool.to_reg(HUGE)
                pool.memset(kz[:], 0.0).then_inc(zeroed, 1)
                pool.memset(va[:, :, :, :, HD:HD + 1], 1.0).then_inc(zeroed, 1)
                step = Steps(pool, p_step, 1)
                with pool.Fori(0, B // 2) as i:
                    for u in range(2):
                        b = 2 * i + u
                        for h in range(H0):
                            n = H0 * b + h
                            pool.wait_ge(d_exp, n + 1)
                            pool.wait_ge(masked, n + 1)
                            pool.wait_ge(m_in[u], 16 * H0 * (i + 1))
                            stand_alone(pool, k)
                            pool.partition_broadcast(mb[:, h % 2, :], mr[32 * h:32 * h + 1, u, :], P).then_inc(mb_ready, 1)
                            pool.wait_ge(mb_ready, 2 * H0 + n + 1)
                            stand_alone(pool, k)
                            pool.affine_select(out=md[:, h % 2, :, :],
                                               in_=mb[:, h % 2, :].rearrange("p (j s) -> p j s", j=NT),
                                               compare_op=ALU.is_ge, fill=huge, base=0,
                                               pattern=[[0, NT], [1, P]], channel_multiplier=-1).then_inc(masked, 1)
                        step.begin(b)
                        pool.wait_ge(v_step, vsteps * b + 11)
                        pool.tensor_tensor(st[:, 6, :], st[:, 4, :], k.neg_half[:, 0:NT * H0], ALU.pow).then_inc(rs_ready, 1)
                        pool.wait_ge(y_ready, b + 3)
                        row = scale_row[:].unsqueeze(1).broadcast_to([P, NT, D])
                        step(pool.tensor_tensor(y[:, u, :, :], y[:, u, :, :], row, ALU.mult))
                        stand_alone(pool, k)
                        xs = k.x[:, bass.ds(NT * b, NT), :]
                        pool.tensor_tensor(xs, xs, y[:, u, :, :], ALU.add).then_inc(x_added, 1)
                        step.end()
                        pool.wait_ge(x_added, b + 3)

            @block.scalar
            def _(act):
                act.sem_inc(ot_ready, 1)
                act.sem_inc(o_ready, 2)
                act.sem_inc(d_exp, 2)
                with act.Fori(0, B // 2) as i:
                    for u in range(2):
                        b = 2 * i + u

                        def decay(h):
                            n = H0 * b + h
                            act.wait_ge(masked, n + 2)
                            act.wait_ge(cv_done, 2 * H0 + n - 1)
                            for j in range(NT):
                                at = acol[:, j, h, bass.ds(b, 1)]
                                last = act.activation(dt[:, h % 2, j, 0:P], md[:, h % 2, j, :], ACT.Exp,
                                                      bias=at, scale=-1.0)
                                if j + 1 < NT:
                                    act.activation(dt[:, h % 2, j, P:S - P * j], mb[:, h % 2, P * (j + 1):S], ACT.Exp,
                                                   bias=at, scale=-1.0)
                            last.then_inc(d_exp, 1)

                        def out_copies(h):
                            n = H0 * b + h
                            act.wait_ge(cv_done, 2 * H0 + n + 1)
                            act.activation(oT[:, h, :], op[0:HD + 1, :], ACT.Copy).then_inc(ot_ready, 1)
                            act.wait_ge(t_done, n + 1)
                            if h == 0:
                                act.wait_ge(y_ready, b + 1)
                            act.activation(o[:, u, :, h, :], tp[h % 2][:], ACT.Copy).then_inc(o_ready, 1)

                        decay(0)
                        decay(1)
                        for h in range(H0):
                            out_copies(h)
                            if h + 2 < H0:
                                decay(h + 2)
                        act.wait_ge(v_step, vsteps * b + 7)
                        act.activation(sq[:], o[:, u, :, :, 0:HD].rearrange("p j h e -> p (j h) e"),
                                       ACT.Square).then_inc(sq_ready, 1)

            @block.vector
            def _(dve):
                dve.sem_inc(y_ready, 2)
                step = Steps(dve, v_step, vsteps)
                with dve.Fori(0, B // 2) as i:
                    for u in range(2):
                        b = 2 * i + u
                        for h in range(H0):
                            n = H0 * b + h
                            dve.wait_ge(d_exp, n + 3)
                            for j in range(NT):
                                w = S - P * j
                                dve.wait_ge(qk_ready, NT * n + j + 1)
                                dve.scalar_tensor_tensor(out=dt[:, h % 2, j, 0:w], in0=qk[j][:, 0:w], scalar=HD ** -0.5,
                                                         in1=dt[:, h % 2, j, 0:w], op0=ALU.mult,
                                                         op1=ALU.mult).then_inc(c_done, 1)
                        step.begin(b)
                        dve.wait_ge(o_ready, 2 + H0 * b + H0)
                        ov = o[:, u, :, :, 0:HD].rearrange("p j h e -> p (j h) e")
                        rows = lambda n: st[:, n, :]
                        wide = lambda n: st[:, n, :].unsqueeze(2).broadcast_to([P, NT * H0, HD])
                        sums = o[:, u, :, :, HD].rearrange("p j h -> p (j h)")
                        step(dve.scalar_tensor_tensor(out=rows(0), in0=sums, scalar=-1.0, in1=sums,
                                                      op0=ALU.mult, op1=ALU.max))
                        step(dve.scalar_tensor_tensor(out=rows(0), in0=rows(0), scalar=0.0,
                                                      in1=exp_nmax[:, :, :, bass.ds(b, 1)].rearrange("p j h e -> p (j h e)"),
                                                      op0=ALU.add, op1=ALU.max))
                        step(dve.tensor_scalar(rows(0), rows(0), EPS_HEAD, None, ALU.add))
                        step(dve.reciprocal(rows(1), rows(0)))
                        step(dve.tensor_reduce(rows(2), ov, AX.X, ALU.add))
                        step(dve.tensor_scalar(rows(2), rows(2), 1.0 / HD, None, ALU.mult))
                        step(dve.tensor_tensor(ov, ov, wide(2), ALU.subtract))
                        step(dve.tensor_tensor(rows(3), rows(1), rows(1), ALU.mult))
                        dve.wait_ge(sq_ready, b + 1)
                        step(dve.tensor_reduce(rows(4), sq[:], AX.X, ALU.add))
                        step(dve.tensor_tensor(rows(4), rows(4), rows(3), ALU.mult))
                        step(dve.tensor_scalar(rows(4), rows(4), 1.0 / HD, EPS_HEAD, ALU.mult, ALU.add))
                        dve.wait_ge(rs_ready, b + 1)
                        step(dve.tensor_tensor(rows(5), rows(1), rows(6), ALU.mult))
                        dve.wait_ge(x_added, b + 1)
                        dve.tensor_tensor(y[:, u, :, :].rearrange("p j (h e) -> p (j h) e", h=H0), ov, wide(5),
                                          ALU.mult).then_inc(y_ready, 1)
                        step.end()


def _gates(nc, k, d, ctx, acol, exp_nmax, m_rows, scale_row):
    def sb(name, shape, dt=F32):
        return ctx.enter_context(nc.sbuf_tensor(f"gate_{name}", shape, dt))

    def sem(name):
        return ctx.enter_context(nc.semaphore(f"gate_{name}"))

    gk = sb("kernels", [P, 3 * DC, GP])
    gkc = sb("context_kernels", [P, DC, GP])
    bias = sb("bias", [P, 1])
    g = sb("preact", [P, S])
    e = sb("e", [P, S])
    lf = sb("log_f", [P, S])
    lfi = sb("log_f_on_i_rows", [P, S])
    zero = sb("zero", [P, S])
    cs = sb("cumsum", [P, S])
    a = sb("a", [P, S])
    m = sb("M", [P, S])
    r = sb("neg_max", [P, S])
    scale_in = sb("scale_in", [P, D])
    gp = ctx.enter_context(nc.psum_tensor("gate_psum", [P, S], F32))
    ap_ = ctx.enter_context(nc.psum_tensor("gate_a_turned", [P, S], F32))
    rp = ctx.enter_context(nc.psum_tensor("gate_r_turned", [P, S], F32))
    kernels_in, bias_in, scale_loaded = sem("kernels_in"), sem("bias_in"), sem("scale_loaded")
    summed, v_step, a_step, blank = sem("summed"), sem("v_step"), sem("a_step"), sem("blank")
    gates_done, moved, spread, turned, cols = (sem("gates_done"), sem("moved"), sem("spread"),
                                               sem("turned"), sem("cols"))
    with nc.Block() as block:
        @block.sync
        def _(sp):
            sp.dma_start(gk[:], d["gate_kernels"].rearrange("(c p) n -> p c n", p=P)).then_inc(kernels_in, 16)
            sp.dma_start(bias[:], d["gate_bias"]).then_inc(bias_in, 16)
            sp.dma_start(scale_in[:], d["outnorm_scale"].rearrange("(a n) -> a n", a=1).broadcast_to([P, D])).then_inc(scale_loaded, 16)
            sp.wait_ge(v_step, 3)
            sp.wait_ge(blank, 2)
            for h in range(H0):
                sp.dma_start(lfi[32 * h:32 * h + B, :], lf[32 * h + B:32 * h + 2 * B, :]).then_inc(moved, 16)
            sp.wait_ge(v_step, 6)
            for h in range(H0):
                sp.dma_start(m_rows[32 * h:32 * h + 1, :, :], m[32 * h:32 * h + B, :]).then_inc(spread, 16)
            sp.wait_ge(spread, 16 * H0)

        @block.gpsimd
        def _(pool):
            pool.memset(lfi[:], 0.0).then_inc(blank, 1)
            pool.memset(zero[:], 0.0).then_inc(blank, 1)

        @block.tensor
        def _(pe):
            pe.wait_ge(summed, 1)
            for b in range(B):
                for n in range(2 * DC):
                    c = n % DC
                    w = gk[:, c, :] if n < DC else gkc[:, c, :]
                    mv = k.xnT if n < DC else k.ctxT
                    last = pe.matmul(gp[:], w[:, B - 1 - b:B - 1 - b + P], mv[:, c, b * S:(b + 1) * S],
                                     start=(b == 0 and n == 0), stop=(b == B - 1 and n == 2 * DC - 1))
            last.then_inc(gates_done, 1)
            pe.wait_ge(v_step, 7)
            for t in range(NT):
                pe.transpose(ap_[:, t * P:(t + 1) * P], a[:, t * P:(t + 1) * P], k.ident[:])
                last = pe.transpose(rp[:, t * P:(t + 1) * P], r[:, t * P:(t + 1) * P], k.ident[:])
            last.then_inc(turned, 1)

        @block.scalar
        def _(act):
            act.wait_ge(bias_in, 16)
            act.wait_ge(gates_done, 1)
            act.activation(g[:], gp[:], ACT.Identity, bias=bias[:]).then_inc(a_step, 1)
            act.wait_ge(v_step, 1)
            act.activation(e[:], e[:], ACT.Exp, scale=-1.0).then_inc(a_step, 1)
            act.wait_ge(v_step, 2)
            act.activation(e[:], e[:], ACT.Ln).then_inc(a_step, 1)
            act.wait_ge(turned, 1)
            act.activation(exp_nmax[:].rearrange("p j h e -> p (j h e)"), rp[:], ACT.Exp)

        @block.vector
        def _(dve):
            dve.wait_ge(kernels_in, 16)
            dve.tensor_tensor(gkc[:], gk[:, DC:2 * DC, :], gk[:, 2 * DC:3 * DC, :], ALU.add).then_inc(summed, 1)
            dve.wait_ge(scale_loaded, 16)
            dve.tensor_scalar(scale_row[:], scale_in[:], k.tg[:, 0:1], None, ALU.mult)
            step = Steps(dve, v_step)
            dve.wait_ge(a_step, 1)
            step(dve.scalar_tensor_tensor(out=e[:], in0=g[:], scalar=-1.0, in1=g[:], op0=ALU.mult, op1=ALU.max))
            dve.wait_ge(a_step, 2)
            step(dve.tensor_scalar(e[:], e[:], 1.0, None, ALU.add))
            dve.wait_ge(a_step, 3)
            step(dve.scalar_tensor_tensor(out=lf[:], in0=g[:], scalar=0.0, in1=e[:], op0=ALU.min, op1=ALU.subtract))
            dve.wait_ge(moved, 16 * H0)
            step(dve.tensor_tensor_scan(cs[:], lfi[:], zero[:], 0.0, ALU.add, ALU.add))
            step(dve.tensor_tensor(a[:], g[:], cs[:], ALU.subtract))
            step(dve.tensor_tensor_scan(m[:], a[:], a[:], LOWEST, ALU.max, ALU.max))
            step(dve.scalar_tensor_tensor(out=r[:], in0=cs[:], scalar=-1.0, in1=m[:], op0=ALU.mult, op1=ALU.subtract))
            dve.wait_ge(turned, 1)
            dve.tensor_copy(acol[:].rearrange("p j h e -> p (j h e)"), ap_[:])


def bitnet_phase(nc, k, d):
    ctx, sb, ps, sem = phase_scope(nc, "bn")
    with ctx:
        w1q = sb("w1q", [P, DC, F0], BF16)
        w2q = sb("w2q", [P, F0 // P, D], BF16)
        b1 = sb("b1_rows", [P, F0])
        b2 = sb("b2_rows", [P, NT, D])
        wcol = sb("weight_scale_cols", [P, 2])
        with ExitStack() as wctx:
            _ternary_weights(nc, k, d, wctx, w1q, w2q, b1, b2, wcol)

        KF = F0 // P
        NS = 9
        stats = sb("stats", [P, NT, 6])
        mv = sb("mean_var", [P, NT, 2])
        col = sb("token_cols", [P, NS, NT])
        xn = sb("xn", [P, NT, D])
        q = sb("q", [P, NT, D], BF16)
        qT = sb("qT", [P, DC, NT, P], BF16)
        h = sb("h", [P, NT, F0])
        hcol = sb("hidden_cols", [P, 4, NT])
        q2 = sb("q2", [P, 2, F0], BF16)
        hT = sb("hT", [P, 2, KF, P], BF16)
        round_col = sb("round_col", [P, 1])
        qTp = ps("qT_psum", [P, DC, NT, P], BF16)
        hp = [ps(f"h_psum{i}", [P, F0]) for i in range(2)]
        hTp = ps("hT_psum", [P, KF, P], BF16)
        op = [ps(f"out_psum{i}", [P, D]) for i in range(2)]

        vq, pq = sem("vector_q_steps"), sem("pool_q_steps")
        VQ, PQ = 8, 3
        turned1, qT_ready, mm1, h_ready, gelu = sem("turned1"), sem("qT_ready"), sem("mm1"), sem("h_ready"), sem("gelu")
        vb, scaled, q2_ready = sem("vector_b_steps"), sem("scaled"), sem("q2_ready")
        turned2, hT_ready, mm2, x_done = sem("turned2"), sem("hT_ready"), sem("mm2"), sem("x_done")
        normed = sem("normed")
        biased, const = sem("biased"), sem("const")
        LAST = B - 1

        def each_batch(eng, before, body, after):
            before()
            body(0, True, False)
            with eng.Fori(1, LAST) as i:
                body(i, False, False)
            body(LAST, False, True)
            after()

        with nc.Block() as block:
            @block.vector
            def _(dve):
                qstep = Steps(dve, vq, VQ)
                bstep = Steps(dve, vb, 4)

                def q_stats(b):
                    qstep.begin(b)
                    for t in range(NT):
                        last = dve.bn_stats(stats[:, t, :], k.x[:, bass.ds(NT * b + t, 1), :])
                    qstep(last)
                    stand_alone(dve, k)
                    for t in range(NT):
                        last = dve.bn_aggr(mv[:, t, :], stats[:, t, :])
                    qstep(last)
                    qstep(dve.tensor_scalar(col[:, 0, :], mv[:, :, 1], EPS_LN, None, ALU.add))

                def q_shift(b):
                    dve.wait_ge(pq, PQ * b + 1)
                    qstep(dve.scalar_tensor_tensor(out=col[:, 2, :], in0=mv[:, :, 0], scalar=-1.0, in1=col[:, 1, :],
                                                   op0=ALU.mult, op1=ALU.mult))

                def q_scale(b):
                    dve.wait_ge(normed, b + 1)
                    qstep(dve.tensor_reduce(col[:, 3, :], xn[:], AX.X, ALU.max, apply_absolute_value=True))
                    qstep(dve.tensor_scalar(col[:, 3, :], col[:, 3, :], EPS_Q, None, ALU.max))
                    qstep(dve.reciprocal(col[:, 4, :], col[:, 3, :]))
                    qstep(dve.tensor_scalar(col[:, 5, :], col[:, 4, :], QB, None, ALU.mult))
                    qstep.end()

                def scale_bias(b, t, first):
                    n = NT * b + t
                    if t == 0:
                        dve.tensor_scalar(col[:, 6, :], col[:, 3, :], wcol[:, 0:1], None, ALU.mult).then_inc(const, 1)
                        dve.wait_ge(const, b + 2)
                    if not first:
                        dve.wait_ge(q2_ready, n - 3)
                    dve.wait_ge(mm1, n + 1)
                    dve.scalar_tensor_tensor(out=h[:, t, :], in0=hp[t % 2][:], scalar=col[:, 6, t:t + 1], in1=b1[:],
                                             op0=ALU.mult, op1=ALU.add).then_inc(h_ready, 1)

                def hidden_scale(n, t):
                    bstep.begin(n)
                    dve.wait_ge(gelu, n + 1)
                    bstep(dve.tensor_reduce(hcol[:, 0, t:t + 1], h[:, t, :], AX.X, ALU.max, apply_absolute_value=True))
                    bstep(dve.tensor_scalar(hcol[:, 0, t:t + 1], hcol[:, 0, t:t + 1], EPS_Q, None, ALU.max))
                    bstep(dve.reciprocal(hcol[:, 1, t:t + 1], hcol[:, 0, t:t + 1]))
                    dve.tensor_scalar(hcol[:, 3, t:t + 1], hcol[:, 0, t:t + 1], wcol[:, 1:2], None, ALU.mult)
                    bstep(dve.tensor_scalar(hcol[:, 2, t:t + 1], hcol[:, 1, t:t + 1], QB, None, ALU.mult))
                    bstep.end()

                def add_out(b, n, t):
                    dve.wait_ge(biased, b + 1)
                    dve.wait_ge(mm2, n + 1)
                    xt = k.x[:, bass.ds(n, 1), :].rearrange("p a e -> p (a e)")
                    dve.scalar_tensor_tensor(out=xt, in0=op[t % 2][:], scalar=hcol[:, 3, t:t + 1], in1=xt,
                                             op0=ALU.mult, op1=ALU.add).then_inc(x_done, 1)

                def before():
                    dve.memset(round_col[:], ROUND).then_inc(const, 1)
                    q_stats(0)
                    q_shift(0)
                    q_scale(0)

                def body(b, first, last):
                    for t in range(NT):
                        n = NT * b + t
                        if not first:
                            add_out(b - 1, n - 4, t)
                        scale_bias(b, t, first)
                        if not (first and t == 0):
                            hidden_scale(n - 1, (t - 1) % NT)
                        if not last:
                            if t == 0:
                                q_stats(b + 1)
                            if t == 1:
                                q_shift(b + 1)
                            if t == 2:
                                dve.wait_ge(mm1, n + 1)
                                q_scale(b + 1)

                def after():
                    hidden_scale(TT - 1, NT - 1)
                    for t in range(NT):
                        add_out(LAST, NT * LAST + t, t)

                each_batch(dve, before, body, after)

            @block.gpsimd
            def _(pool):
                pstep = Steps(pool, pq, PQ)

                def q_rstd(b):
                    pstep.begin(b)
                    pool.wait_ge(vq, VQ * b + 3)
                    pstep(pool.tensor_tensor(col[:, 1, :], col[:, 0, :], k.neg_half[:, 0:NT], ALU.pow))

                def add_bias(b):
                    pool.wait_ge(normed, b + 1)
                    stand_alone(pool, k)
                    xs = k.x[:, bass.ds(NT * b, NT), :]
                    pool.tensor_tensor(xs, xs, b2[:], ALU.add).then_inc(biased, 1)

                def q_round(b, first):
                    pool.wait_ge(vq, VQ * b + 8)
                    stand_alone(pool, k)
                    for t in range(NT):
                        last = pool.tensor_scalar(xn[:, t, :], xn[:, t, :], col[:, 5, t:t + 1], ROUND, ALU.mult, ALU.add)
                    pstep(last)
                    if not first:
                        pool.wait_ge(turned1, b)
                    stand_alone(pool, k)
                    pstep(pool.tensor_scalar(q[:], xn[:], -ROUND, 1.0, ALU.add, ALU.mult))
                    pstep.end()

                def hidden_round(n, t, early):
                    pool.wait_ge(scaled, n + 1)
                    if not early:
                        pool.wait_ge(turned2, n - 1)
                    stand_alone(pool, k)
                    pool.tensor_scalar(q2[:, t % 2, :], h[:, t, :], -ROUND, 1.0, ALU.add, ALU.mult).then_inc(q2_ready, 1)

                def before():
                    q_rstd(0)
                    add_bias(0)
                    q_round(0, True)

                def body(b, first, last):
                    for t in range(NT):
                        n = NT * b + t
                        if not (first and t == 0):
                            hidden_round(n - 1, (t - 1) % NT, first and t < 3)
                        if not last:
                            if t == 0:
                                q_rstd(b + 1)
                            if t == 1:
                                add_bias(b + 1)
                            if t == 2:
                                q_round(b + 1, False)

                def after():
                    hidden_round(TT - 1, NT - 1, False)

                each_batch(pool, before, body, after)

            @block.tensor
            def _(pe):
                def first_product(b, t, first):
                    n = NT * b + t
                    if t == 0:
                        pe.wait_ge(pq, PQ * b + 3)
                        for c in range(DC):
                            for j in range(NT):
                                last = pe.transpose(qTp[:, c, j, :], q[:, j, c * P:(c + 1) * P], k.identb[:])
                        last.then_inc(turned1, 1)
                        pe.wait_ge(qT_ready, b + 1)
                    if not (first and t < 2):
                        pe.wait_ge(h_ready, n - 1)
                    for m in range(F0 // S):
                        for c in range(DC):
                            last = pe.matmul(hp[t % 2][:, m * S:(m + 1) * S], qT[:, c, t, :],
                                             w1q[:, c, m * S:(m + 1) * S], start=(c == 0), stop=(c == DC - 1))
                    last.then_inc(mm1, 1)

                def turn(n, t, early):
                    pe.wait_ge(q2_ready, n + 1)
                    if not early:
                        pe.wait_ge(hT_ready, n)
                    for c in range(KF):
                        last = pe.transpose(hTp[:, c, :], q2[:, t % 2, c * P:(c + 1) * P], k.identb[:])
                    last.then_inc(turned2, 1)

                def second_product(n, t, early):
                    pe.wait_ge(hT_ready, n + 1)
                    if not early:
                        pe.wait_ge(x_done, n - 1)
                    for c in range(KF):
                        last = pe.matmul(op[t % 2][:], hT[:, t % 2, c, :], w2q[:, c, :],
                                         start=(c == 0), stop=(c == KF - 1))
                    last.then_inc(mm2, 1)

                def body(b, first, last):
                    for t in range(NT):
                        n = NT * b + t
                        first_product(b, t, first)
                        if not (first and t < 3):
                            second_product(n - 3, (t - 3) % NT, first)
                        if not (first and t < 2):
                            turn(n - 2, (t - 2) % NT, first and t == 2)

                def after():
                    second_product(TT - 3, NT - 3, False)
                    turn(TT - 2, NT - 2, False)
                    second_product(TT - 2, NT - 2, False)
                    turn(TT - 1, NT - 1, False)
                    second_product(TT - 1, NT - 1, False)

                each_batch(pe, lambda: None, body, after)

            @block.scalar
            def _(act):
                def copy_qT(b):
                    act.wait_ge(turned1, b + 1)
                    act.activation(qT[:], qTp[:], ACT.Copy).then_inc(qT_ready, 1)

                def normalize(b):
                    act.wait_ge(vq, VQ * b + 4)
                    for t in range(NT):
                        last = act.activation(xn[:, t, :], k.x[:, bass.ds(NT * b + t, 1), :].rearrange("p a e -> p (a e)"),
                                              ACT.Identity, bias=col[:, 2, t:t + 1], scale=col[:, 1, t:t + 1])
                    last.then_inc(normed, 1)

                def do_gelu(n, t):
                    act.wait_ge(h_ready, n + 1)
                    act.activation(h[:, t, :], h[:, t, :], ACT.Gelu).then_inc(gelu, 1)

                def do_scale(n, t):
                    act.wait_ge(vb, 4 * n + 4)
                    act.activation(h[:, t, :], h[:, t, :], ACT.Identity, scale=hcol[:, 2, t:t + 1],
                                   bias=round_col[:]).then_inc(scaled, 1)

                def copy_hT(n, t, early):
                    act.wait_ge(turned2, n + 1)
                    if not early:
                        act.wait_ge(mm2, n - 1)
                    act.activation(hT[:, t % 2, :, :], hTp[:], ACT.Copy).then_inc(hT_ready, 1)

                def body(b, first, last):
                    for t in range(NT):
                        n = NT * b + t
                        if t == 0:
                            copy_qT(b)
                        do_gelu(n, t)
                        if not (first and t == 0):
                            do_scale(n - 1, (t - 1) % NT)
                        if not (first and t < 2):
                            copy_hT(n - 2, (t - 2) % NT, first)
                        if not last and t == 1:
                            act.wait_ge(turned1, b + 1)
                            normalize(b + 1)

                def after():
                    do_scale(TT - 1, NT - 1)
                    copy_hT(TT - 2, NT - 2, False)
                    copy_hT(TT - 1, NT - 1, False)

                each_batch(act, lambda: normalize(0), body, after)


def _ternary_weights(nc, k, d, ctx, w1q, w2q, b1, b2, wcol):
    def sb(name, shape, dt=F32):
        return ctx.enter_context(nc.sbuf_tensor(f"tw_{name}", shape, dt))

    def sem(name):
        return ctx.enter_context(nc.semaphore(f"tw_{name}"))

    N = F0 * D
    w = [sb("w1", [P, N // P]), sb("w2", [P, N // P])]
    part = sb("abs_sums", [P, 2])
    ones = sb("ones", [P, P])
    ws = sb("scales", [P, 2])
    inv = sb("inverse_scales", [P, 2])
    b2_in = sb("b2_in", [P, D])
    total = ctx.enter_context(nc.psum_tensor("tw_total", [P, 2], F32))
    w_in, b_in, v_step, totals = [sem("w1_in"), sem("w2_in")], sem("b_in"), sem("v_step"), sem("totals")
    with nc.Block() as block:
        @block.sync
        def _(sp):
            sp.dma_start(w[0][:].rearrange("p (c f) -> p c f", c=DC),
                         d["W1T"].rearrange("(c p) f -> p c f", p=P)).then_inc(w_in[0], 16)
            sp.dma_start(w[1][:].rearrange("p (c f) -> p c f", c=F0 // P),
                         d["W2T"].rearrange("(c p) f -> p c f", p=P)).then_inc(w_in[1], 16)
            sp.dma_start(b1[:], d["b1"].rearrange("(a n) -> a n", a=1).broadcast_to([P, F0])).then_inc(b_in, 16)
            sp.dma_start(b2_in[:], d["b2"].rearrange("(a n) -> a n", a=1).broadcast_to([P, D])).then_inc(b_in, 16)
            sp.wait_ge(b_in, 32)

        @block.tensor
        def _(pe):
            pe.wait_ge(v_step, 3)
            pe.matmul(total[:], ones[:], part[:], start=True, stop=True).then_inc(totals, 1)

        @block.vector
        def _(dve):
            step = Steps(dve, v_step)
            step(dve.memset(ones[:], 1.0))
            for n in range(2):
                dve.wait_ge(w_in[n], 16)
                step(dve.tensor_reduce(part[:, n:n + 1], w[n][:], AX.X, ALU.add, apply_absolute_value=True))
            dve.wait_ge(totals, 1)
            step(dve.tensor_scalar(ws[:], total[:], 1.0 / N, EPS_Q, ALU.mult, ALU.max))
            step(dve.reciprocal(inv[:], ws[:]))
            dve.tensor_scalar(wcol[:, 0:1], ws[:, 0:1], 1.0 / QB, None, ALU.mult)
            dve.tensor_scalar(wcol[:, 1:2], ws[:, 1:2], 1.0 / QB, k.tg[:, 1:2], ALU.mult, ALU.mult)
            for n in range(2):
                step(dve.tensor_scalar(w[n][:], w[n][:], inv[:, n:n + 1], ROUND, ALU.mult, ALU.add))
                step(dve.tensor_scalar(w[n][:], w[n][:], ROUND, 1.0, ALU.subtract, ALU.min))
                out = (w1q, w2q)[n][:].rearrange("p c f -> p (c f)")
                step(dve.tensor_scalar(out, w[n][:], -1.0, None, ALU.max))
            dve.wait_ge(b_in, 32)
            for t in range(NT):
                dve.tensor_scalar(b2[:, t, :], b2_in[:], k.tg[:, 1:2], None, ALU.mult)


def attention_phase(nc, k, d):
    ctx, sb, ps, sem = phase_scope(nc, "at")
    PAIRS = H1 // 2
    NSTEP = B * PAIRS
    TI = 2 * NT
    with ctx:
        wqkv = sb("w_qkv", [P, 2, DC, 3 * P])
        w0 = sb("w_0", [P, 2, D])
        qs = sb("q_stack", [P, 2, 2, S], F32R)
        kh = sb("k_hi_twice", [P, 2, 2, S], F32R)
        kl = sb("k_lo_twice", [P, 2, 2, S], F32R)
        vT = sb("v_T", [P, S])
        v = sb("v", [P, 2, NT, P])
        pr = sb("probs", [P, 4, S])
        pT = sb("probs_T", [P, 2, 2, NT, S])
        oT = sb("o_T", [P, S])
        nmax = sb("neg_max", [P, TI])
        sums = sb("sums", [P, TI])
        rinv = sb("inverse_sums", [P, TI])
        jp = [ps(f"proj{i}", [P, S]) for i in range(2)]
        sp_ = [ps(f"scores{i}", [P, S]) for i in range(2)]
        tp = [ps(f"turned{i}", [P, NT, P]) for i in range(2)]
        op = ps("out", [P, S])
        wp = ps("w0_out", [P, S])

        wqkv_in, w0_in = [sem("wqkv_in0"), sem("wqkv_in1")], [sem("w0_in0"), sem("w0_in1")]
        q_psum, k_psum, v_psum, vt_psum = sem("q_psum"), sem("k_psum"), sem("v_psum"), sem("vt_psum")
        q_hi, q_lo, k_hi, k_lo = sem("q_hi"), sem("q_lo"), sem("k_hi"), sem("k_lo")
        k_twice = [sem("k_twice0"), sem("k_twice1")]
        vT_sb, v_sb = sem("vT_sb"), sem("v_sb")
        scored, maxed, exped, inverted = sem("scored"), sem("maxed"), sem("exped"), sem("inverted")
        normed, turned, even_copied, odd_copied = sem("normed"), sem("turned"), sem("even_copied"), sem("odd_copied")
        av, o_copied, w0_done, x_added = sem("av"), sem("o_copied"), sem("w0_done"), sem("x_added")

        def steps(eng, before, body, after):
            before()
            body(0, 0, True, False)
            with eng.Fori(0, (NSTEP - 2) // 2) as i:
                body(2 * i + 1, 1, False, False)
                body(2 * i + 2, 0, False, False)
            body(NSTEP - 1, 1, False, True)
            after()

        HALVES = (slice(0, HD), slice(HD, P))

        with nc.Block() as block:
            @block.sync
            def _(sp):
                def load_qkv(s, u):
                    src = d["w_qkv"][bass.ds(s % PAIRS, 1), :, :].rearrange("a (c p) n -> p (a c) n", p=P)
                    sp.dma_start(wqkv[:, u, :, :], src).then_inc(wqkv_in[u], 16)

                def load_w0(s, u):
                    src = d["w_0"][bass.ds(s % PAIRS, 1), :, :].rearrange("a p n -> (a p) n")
                    sp.dma_start(w0[:, u, :], src).then_inc(w0_in[u], 16)

                def k_again(s, u):
                    sp.wait_ge(k_hi, s + 1)
                    for hd in range(2):
                        sp.dma_start(kh[HALVES[1 - hd], u, hd, :].bitcast(F32),
                                     kh[HALVES[hd], u, hd, :].bitcast(F32)).then_inc(k_twice[u], 16)
                    sp.wait_ge(k_lo, s + 1)
                    for hd in range(2):
                        sp.dma_start(kl[HALVES[1 - hd], u, hd, :].bitcast(F32),
                                     kl[HALVES[hd], u, hd, :].bitcast(F32)).then_inc(k_twice[u], 16)

                def before():
                    for n in range(2):
                        load_qkv(n, n)
                        load_w0(n, n)
                    k_again(0, 0)
                    sp.wait_ge(v_psum, 1)
                    load_qkv(2, 0)

                def body(s, u, first, last):
                    if last:
                        return
                    k_again(s + 1, 1 - u)
                    sp.wait_ge(v_psum, s + 2)
                    load_qkv(s + 3, 1 - u)
                    if not first:
                        sp.wait_ge(w0_done, s)
                        load_w0(s + 1, 1 - u)

                steps(sp, before, body, lambda: (sp.wait_ge(wqkv_in[0], 16 * (NSTEP // 2 + 1)),
                                                 sp.wait_ge(wqkv_in[1], 16 * (NSTEP // 2 + 1))))

            @block.tensor
            def _(pe):
                def project(s, u, part, bank, done):
                    at = bass.ds(S * (s // PAIRS), S)
                    src = k.xnT if part == 0 else k.ctxT
                    for c in range(DC):
                        last = pe.matmul(jp[bank][:], wqkv[:, u, c, part * P:(part + 1) * P], src[:, c, at],
                                         start=(c == 0), stop=(c == DC - 1))
                    last.then_inc(done, 1)

                def project_q(s, u, early):
                    pe.wait_ge(wqkv_in[u], 16 * (s // 2 + 1))
                    if not early:
                        pe.wait_ge(vT_sb, s)
                    project(s, u, 0, 0, q_psum)

                def project_k(s, u, early):
                    if not early:
                        pe.wait_ge(v_sb, s)
                    project(s, u, 1, 1, k_psum)

                def project_v(s, u):
                    pe.wait_ge(q_hi, s + 1)
                    pe.wait_ge(q_lo, s + 1)
                    project(s, u, 2, 0, v_psum)

                def turn_v(s):
                    pe.wait_ge(k_hi, s + 1)
                    pe.wait_ge(k_lo, s + 1)
                    pe.wait_ge(vT_sb, s + 1)
                    for j in range(NT):
                        last = pe.transpose(jp[1][:, j * P:(j + 1) * P], vT[:, j * P:(j + 1) * P], k.ident[:])
                    last.then_inc(vt_psum, 1)

                def scores(s, u, i, first):
                    hd, m = i // NT, i % NT
                    if i == 0:
                        pe.wait_ge(q_hi, s + 1)
                        pe.wait_ge(q_lo, s + 1)
                        pe.wait_ge(k_twice[u], 64 * (s // 2 + 1))
                    if not (first and i < 2):
                        pe.wait_ge(exped, TI * s + i - 1)
                    lhs = qs[:, u, hd, m * P:(m + 1) * P]
                    pe.matmul(sp_[i % 2][:], lhs, kh[:, u, hd, :], start=True, stop=False)
                    pe.matmul(sp_[i % 2][:], lhs, kl[:, u, hd, :], start=False, stop=True).then_inc(scored, 1)

                def turn(s, i, first):
                    pe.wait_ge(normed, TI * s + i + 1)
                    if not (first and i < 2):
                        pe.wait_ge((even_copied, odd_copied)[i % 2], NT * s + i // 2)
                    for j in range(NT):
                        last = pe.transpose(tp[i % 2][:, j, :], pr[:, i % 4, j * P:(j + 1) * P], k.ident[:])
                    last.then_inc(turned, 1)

                def weigh_v(s, u):
                    pe.wait_ge(even_copied, NT * (s + 1))
                    pe.wait_ge(odd_copied, NT * (s + 1))
                    pe.wait_ge(v_sb, s + 1)
                    pe.wait_ge(x_added, s + 1)
                    for j in range(NT):
                        for hd in range(2):
                            last = pe.matmul(op[HALVES[hd], :], v[:, u, j, HALVES[hd]], pT[:, u, hd, j, :],
                                             start=(j == 0), stop=(j == NT - 1))
                    last.then_inc(av, 1)

                def output(s, u):
                    pe.wait_ge(o_copied, s + 1)
                    pe.wait_ge(w0_in[u], 16 * (s // 2 + 1))
                    for m in range(NT):
                        bank = (wp, op)[m // 2]
                        last = pe.matmul(bank[:, (m % 2) * D:(m % 2 + 1) * D], oT[:, m * P:(m + 1) * P], w0[:, u, :],
                                         start=True, stop=True)
                    last.then_inc(w0_done, 1)

                def before():
                    project_q(0, 0, True)
                    project_k(0, 0, True)
                    project_v(0, 0)
                    turn_v(0)

                def body(s, u, first, last):
                    for i in range(TI):
                        scores(s, u, i, first)
                        if i >= 3:
                            turn(s, i - 3, first)
                        elif not first:
                            turn(s - 1, i - 3 + TI, False)
                        if not last:
                            if i == 0:
                                project_q(s + 1, 1 - u, False)
                            if i == 2:
                                project_k(s + 1, 1 - u, False)
                            if i == 5:
                                project_v(s + 1, 1 - u)
                            if i == 7:
                                turn_v(s + 1)
                        if not first:
                            if i == 4:
                                weigh_v(s - 1, 1 - u)
                            if i == 6:
                                output(s - 1, 1 - u)

                def after():
                    for i in range(TI - 3, TI):
                        turn(NSTEP - 1, i, False)
                    weigh_v(NSTEP - 1, 1)
                    output(NSTEP - 1, 1)

                steps(pe, before, body, after)

            @block.scalar
            def _(act):
                def hi(s, u, psum_ready, bank, dst, done, scale):
                    act.wait_ge(psum_ready, s + 1)
                    for hd in range(2):
                        last = act.activation(dst[HALVES[hd], u, hd, :], jp[bank][HALVES[hd], :], ACT.Copy, scale=scale)
                    last.then_inc(done, 1)

                def exponent(s, i, first):
                    act.wait_ge(maxed, TI * s + i + 1)
                    if not (first and i < 4):
                        act.wait_ge(turned, TI * s + i - 3)
                    act.activation(pr[:, i % 4, :], sp_[i % 2][:], ACT.Exp, bias=nmax[:, i:i + 1],
                                   accum_out=sums[:, i:i + 1]).then_inc(exped, 1)

                def copy_turned(s, u, i):
                    act.wait_ge(turned, TI * s + i + 1)
                    m = i % NT
                    act.activation(pT[:, u, i // NT, :, m * P:(m + 1) * P], tp[i % 2][:], ACT.Copy).then_inc(even_copied, 1)

                def copy_vT(s):
                    act.wait_ge(v_psum, s + 1)
                    act.activation(vT[:], jp[0][:], ACT.Copy).then_inc(vT_sb, 1)

                def copy_o(s):
                    act.wait_ge(av, s + 1)
                    act.activation(oT[:], op[:], ACT.Copy).then_inc(o_copied, 1)

                def before():
                    hi(0, 0, q_psum, 0, qs, q_hi, HD ** -0.5)
                    hi(0, 0, k_psum, 1, kh, k_hi, 1.0)
                    copy_vT(0)

                def body(s, u, first, last):
                    for i in range(TI):
                        exponent(s, i, first)
                        if i % 2:
                            if i >= 3:
                                copy_turned(s, u, i - 3)
                            elif not first:
                                copy_turned(s - 1, 1 - u, i - 3 + TI)
                        if not last:
                            if i == 0:
                                hi(s + 1, 1 - u, q_psum, 0, qs, q_hi, HD ** -0.5)
                            if i == 2:
                                hi(s + 1, 1 - u, k_psum, 1, kh, k_hi, 1.0)
                            if i == 6:
                                copy_vT(s + 1)
                        if not first and i == 5:
                            copy_o(s - 1)

                def after():
                    copy_turned(NSTEP - 1, 1, TI - 2)
                    copy_o(NSTEP - 1)

                steps(act, before, body, after)

            @block.vector
            def _(dve):
                def lo(s, u, psum_ready, hi_ready, bank, his, dst, flip, done, scale):
                    dve.wait_ge(hi_ready, s + 1)
                    for hd in range(2):
                        to = HALVES[1 - hd] if flip else HALVES[hd]
                        last = dve.scalar_tensor_tensor(out=dst[to, u, hd, :], in0=jp[bank][HALVES[hd], :], scalar=scale,
                                                        in1=his[HALVES[hd], u, hd, :].bitcast(F32),
                                                        op0=ALU.mult, op1=ALU.subtract)
                    last.then_inc(done, 1)

                def row_max(s, i):
                    dve.wait_ge(scored, TI * s + i + 1)
                    dve.tensor_reduce(nmax[:, i:i + 1], sp_[i % 2][:], AX.X, ALU.max, negate=True).then_inc(maxed, 1)

                def invert(s, i):
                    dve.wait_ge(exped, TI * s + i + 1)
                    dve.reciprocal(rinv[:, i:i + 1], sums[:, i:i + 1]).then_inc(inverted, 1)

                def copy_turned(s, u, i):
                    dve.wait_ge(turned, TI * s + i + 1)
                    m = i % NT
                    dve.tensor_copy(pT[:, u, i // NT, :, m * P:(m + 1) * P], tp[i % 2][:]).then_inc(odd_copied, 1)

                def copy_v(s, u, early):
                    dve.wait_ge(vt_psum, s + 1)
                    if not early:
                        dve.wait_ge(av, s - 1)
                    dve.tensor_copy(v[:, u, :, :].rearrange("p j e -> p (j e)"), jp[1][:]).then_inc(v_sb, 1)

                def add_out(s):
                    dve.wait_ge(w0_done, s + 1)
                    for m in range(2):
                        xs = k.x[:, bass.ds(NT * (s // PAIRS) + 2 * m, 2), :]
                        bank = (wp, op)[m][:].rearrange("p (t e) -> p t e", t=2)
                        last = dve.scalar_tensor_tensor(out=xs, in0=bank, scalar=k.tg[:, 2:3], in1=xs,
                                                        op0=ALU.mult, op1=ALU.add)
                    last.then_inc(x_added, 1)
                    dve.wait_ge(x_added, s + 2)

                def before():
                    dve.sem_inc(x_added, 1)
                    lo(0, 0, q_psum, q_hi, 0, qs, qs, True, q_lo, HD ** -0.5)
                    lo(0, 0, k_psum, k_hi, 1, kh, kl, False, k_lo, 1.0)
                    copy_v(0, 0, True)

                def body(s, u, first, last):
                    for i in range(TI):
                        row_max(s, i)
                        if i > 0:
                            invert(s, i - 1)
                        elif not first:
                            invert(s - 1, TI - 1)
                        if i % 2 == 0:
                            if i >= 4:
                                copy_turned(s, u, i - 3)
                            elif not first:
                                copy_turned(s - 1, 1 - u, i - 3 + TI)
                        if not last:
                            if i == 1:
                                lo(s + 1, 1 - u, q_psum, q_hi, 0, qs, qs, True, q_lo, HD ** -0.5)
                            if i == 3:
                                lo(s + 1, 1 - u, k_psum, k_hi, 1, kh, kl, False, k_lo, 1.0)
                        if not first and i == 7:
                            add_out(s - 1)
                        if not last and i == 7:
                            copy_v(s + 1, 1 - u, first)

                def after():
                    invert(NSTEP - 1, TI - 1)
                    copy_turned(NSTEP - 1, 1, TI - 3)
                    copy_turned(NSTEP - 1, 1, TI - 1)
                    add_out(NSTEP - 1)

                steps(dve, before, body, after)

            @block.gpsimd
            def _(pool):
                def divide(s, i):
                    pool.wait_ge(inverted, TI * s + i + 1)
                    stand_alone(pool, k)
                    pool.tensor_scalar(pr[:, i % 4, :], pr[:, i % 4, :], rinv[:, i:i + 1], 1.0,
                                       ALU.mult, ALU.mult).then_inc(normed, 1)

                def body(s, u, first, last):
                    for i in range(TI):
                        if i > 0:
                            divide(s, i - 1)
                        elif not first:
                            divide(s - 1, TI - 1)

                steps(pool, lambda: None, body, lambda: divide(NSTEP - 1, TI - 1))


def router_phase(nc, k, d, weights):
    ctx, sb, ps, sem = phase_scope(nc, "ro")
    with ctx:
        gw = sb("gate_w", [P, DC, NE])
        lT = sb("logits_T", [NE, B, S])
        lg = sb("logits", [P, TT, NE])
        top = sb("top", [P, TT, 8])
        idx = sb("index", [P, TT, 8], U32)
        idf = sb("index_f32", [P, TT, 2])
        ids = sb("expert_ids", [P, NE])
        cols = sb("cols", [P, 3, TT])
        one = sb("one_hot", [P, TT, NE])
        lp = [ps(f"logits_psum{i}", [P, S]) for i in range(2)]
        tp = ps("turned", [P, TT, NE])
        gw_in, logits, copied, turned, ids_made, v_step, ex = (sem("gw_in"), sem("logits_done"), sem("copied"),
                                                             sem("all_turned"), sem("ids_made"), sem("v_step"), sem("ex"))
        with nc.Block() as block:
            @block.sync
            def _(sp):
                sp.dma_start(gw[:], d["gate_w"].rearrange("(c p) e -> p c e", p=P)).then_inc(gw_in, 16)

            @block.gpsimd
            def _(pool):
                pool.iota(ids[:], [[1, NE]], base=0, channel_multiplier=0,
                          allow_small_or_imprecise_dtypes=True).then_inc(ids_made, 1)

            @block.tensor
            def _(pe):
                pe.wait_ge(gw_in, 16)
                for b in range(B):
                    if b >= 2:
                        pe.wait_ge(copied, b - 1)
                    for c in range(DC):
                        last = pe.matmul(lp[b % 2][0:NE, :], gw[:, c, :], k.xnT[:, c, b * S:(b + 1) * S],
                                         start=(c == 0), stop=(c == DC - 1))
                    last.then_inc(logits, 1)
                pe.wait_ge(copied, B)
                for t in range(TT):
                    last = pe.transpose(tp[:, t, :], lT[:, t // NT, (t % NT) * P:(t % NT + 1) * P], k.ident[0:NE, 0:NE])
                last.then_inc(turned, 1)

            @block.scalar
            def _(act):
                for b in range(B):
                    act.wait_ge(logits, b + 1)
                    act.activation(lT[:, b, :], lp[b % 2][0:NE, :], ACT.Copy).then_inc(copied, 1)
                act.wait_ge(v_step, 4)
                act.activation(cols[:, 0, :], cols[:, 0, :], ACT.Exp).then_inc(ex, 1)

            @block.vector
            def _(dve):
                step = Steps(dve, v_step)
                dve.wait_ge(turned, 1)
                step(dve.tensor_copy(lg[:], tp[:]))
                for t in range(TT):
                    last = dve.max(top[:, t, :], lg[:, t, :])
                step(last)
                for t in range(TT):
                    last = dve.max_index(idx[:, t, :], top[:, t, :], lg[:, t, :])
                step(last)
                step(dve.tensor_tensor(cols[:, 0, :], top[:, :, 1], top[:, :, 0], ALU.subtract))
                step(dve.tensor_copy(idf[:], idx[:, :, 0:2]))
                dve.wait_ge(ex, 1)
                step(dve.tensor_scalar(cols[:, 2, :], cols[:, 0, :], 1.0, None, ALU.add))
                step(dve.reciprocal(cols[:, 1, :], cols[:, 2, :]))
                step(dve.tensor_scalar(cols[:, 1, :], cols[:, 1, :], k.tg[:, 3:4], None, ALU.mult))
                step(dve.tensor_tensor(cols[:, 2, :], cols[:, 0, :], cols[:, 1, :], ALU.mult))
                dve.wait_ge(ids_made, 1)
                wide = lambda x: x.unsqueeze(2).broadcast_to([P, TT, NE])
                ids_w = ids[:].unsqueeze(1).broadcast_to([P, TT, NE])
                for n, out in ((0, weights), (1, one)):
                    step(dve.tensor_tensor(out[:], ids_w, wide(idf[:, :, n]), ALU.is_equal))
                    step(dve.tensor_tensor(out[:], out[:], wide(cols[:, 1 + n, :]), ALU.mult))
                dve.tensor_tensor(weights[:], weights[:], one[:], ALU.add)


def experts_phase(nc, k, d, weights):
    ctx, sb, ps, sem = phase_scope(nc, "ex")
    with ctx:
        w1 = sb("w1", [P, 2, DC, FE])
        w2 = sb("w2", [P, 2, FC, D])
        hT = sb("h_T", [P, 2, FC, S])
        hp = [ps(f"h_psum{i}", [P, S]) for i in range(FC)]
        yp = [ps(f"y_psum{i}", [P, 2, D]) for i in range(2)]
        w_in = [sem("w_in0"), sem("w_in1")]
        hidden, silu, y_done, x_done = sem("hidden"), sem("silu"), sem("y_done"), sem("x_done")

        def steps(eng, body):
            with eng.Fori(0, NE // 2) as i:
                for ue in range(2):
                    e = 2 * i + ue
                    with eng.Fori(0, B // 2) as j:
                        for ub in range(2):
                            body(e, ue, 2 * j + ub, ub, i)

        with nc.Block() as block:
            @block.sync
            def _(sp):
                with sp.Fori(0, NE // 2) as i:
                    for u in range(2):
                        e = 2 * i + u
                        sp.wait_ge(y_done, 2 * B * (e + 1))
                        sp.dma_start(w1[:, u, :, :], d["w1"][bass.ds(e, 1), :, :].rearrange("a (c p) n -> p (a c) n", p=P)).then_inc(w_in[u], 16)
                        sp.dma_start(w2[:, u, :, :], d["w2"][bass.ds(e, 1), :, :].rearrange("a (c p) n -> p (a c) n", p=P)).then_inc(w_in[u], 16)

            @block.tensor
            def _(pe):
                pe.sem_inc(y_done, 4 * B)

                def body(e, ue, b, ub, i):
                    s = B * e + b
                    pe.wait_ge(w_in[ue], 32 * (i + 1))
                    for f in range(FC):
                        pe.wait_ge(silu, FC * s + f + 1)
                        for c in range(DC):
                            last = pe.matmul(hp[f][:], w1[:, ue, c, f * P:(f + 1) * P], k.xnT[:, c, bass.ds(S * b, S)],
                                             start=(c == 0), stop=(c == DC - 1))
                        last.then_inc(hidden, 1)
                    pe.wait_ge(silu, FC * (s + 1) + FC)
                    for m in range(NT):
                        if m % 2 == 0:
                            pe.wait_ge(x_done, 2 * s + m // 2 + 1)
                        for f in range(FC):
                            last = pe.matmul(yp[m // 2][:, m % 2, :], hT[:, ub, f, m * P:(m + 1) * P], w2[:, ue, f, :],
                                             start=(f == 0), stop=(f == FC - 1))
                        if m % 2:
                            last.then_inc(y_done, 1)

                steps(pe, body)

            @block.scalar
            def _(act):
                act.sem_inc(silu, FC)

                def body(e, ue, b, ub, i):
                    s = B * e + b
                    act.wait_ge(y_done, 4 * B + 2 * s - 2)
                    for f in range(FC):
                        act.wait_ge(hidden, FC * s + f + 1)
                        act.activation(hT[:, ub, f, :], hp[f][:], ACT.Silu).then_inc(silu, 1)

                steps(act, body)

            @block.vector
            def _(dve):
                dve.sem_inc(x_done, 2)

                def body(e, ue, b, ub, i):
                    s = B * e + b
                    for m in range(NT):
                        if m % 2 == 0:
                            dve.wait_ge(y_done, 4 * B + 2 * s + m // 2 + 1)
                        n = NT * b + m
                        xt = k.x[:, bass.ds(n, 1), :].rearrange("p a e -> p (a e)")
                        at = weights[:, bass.ds(n, 1), bass.ds(e, 1)].rearrange("p a e -> p (a e)")
                        last = dve.scalar_tensor_tensor(out=xt, in0=yp[m // 2][:, m % 2, :], scalar=at, in1=xt,
                                                        op0=ALU.mult, op1=ALU.add)
                        if m % 2:
                            last.then_inc(x_done, 1)

                steps(dve, body)


def store_phase(nc, k, d):
    ctx, sb, ps, sem = phase_scope(nc, "st")
    with ctx:
        stored = sem("stored")
        with nc.Block() as block:
            @block.sync
            def _(sp):
                sp.dma_start(d["out"].rearrange("(t p) d -> p t d", p=P), k.x[:]).then_inc(stored, 16)
                sp.wait_ge(stored, 16)


def build(nc, d, phases="abcd"):
    with ExitStack() as ctx:
        k = Core(nc, ctx)
        load_phase(nc, k, d)
        if "a" in phases:
            norm_phase(nc, k, "n0")
            mlstm_phase(nc, k, d)
        if "b" in phases:
            bitnet_phase(nc, k, d)
        if "c" in phases:
            norm_phase(nc, k, "n2")
            attention_phase(nc, k, d)
        if "d" in phases:
            norm_phase(nc, k, "n3")
            with nc.sbuf_tensor("expert_weights", [P, TT, NE], F32) as weights:
                router_phase(nc, k, d, weights)
                experts_phase(nc, k, d, weights)
        store_phase(nc, k, d)


def _layout(i):
    import numpy as np

    def flip(a):
        return np.ascontiguousarray(np.asarray(a).T)

    x = np.asarray(i["x"]).reshape(B * S, D)
    context = np.asarray(i["ctx_1024"]).reshape(B * S, D)
    gk = np.zeros((3 * D, GP), np.float32)
    gb = np.zeros((H0, 32), np.float32)
    for h in range(H0):
        gk[:, 32 * h + B - 1] = i["L0_xattn_igate_kernel"][:, h]
        gk[:, 32 * h + 2 * B - 1] = i["L0_xattn_fgate_kernel"][:, h]
        gb[h, 0:B] = i["L0_xattn_igate_bias"][h]
        gb[h, B:2 * B] = i["L0_xattn_fgate_bias"][h]
    wq = np.asarray(i["L1_xattn_Wq"]).reshape(HD, H1 // 2, 2, D)
    wkv = np.asarray(i["L1_xattn_Wkv"]).reshape(HD, 2, H1 // 2, 2, D)
    parts = [p.transpose(1, 3, 2, 0).reshape(H1 // 2, D, P) for p in (wq, wkv[:, 0], wkv[:, 1])]
    return {
        "x": x, "ctx": context, "ctxT": flip(context), "g_xattn": i["g_xattn"], "g_ffn": i["g_ffn"],
        "gate_kernels": gk, "gate_bias": gb.reshape(P, 1), "outnorm_scale": i["L0_xattn_outnorm_scale"],
        "W1T": flip(i["L0_ffn_W1"]), "W2T": flip(i["L0_ffn_W2"]), "b1": i["L0_ffn_b1"], "b2": i["L0_ffn_b2"],
        "w_qkv": np.concatenate(parts, axis=2), "w_0": flip(i["L1_xattn_W0"]).reshape(H1 // 2, P, D),
        "gate_w": i["L1_ffn_gate_w"], "w1": i["L1_ffn_w1"], "w2": i["L1_ffn_w2"],
    }


def kernel(**inputs):
    import numpy as np
    import concourse.bacc as bacc
    from concourse.bass_utils import run_bass_kernel_spmd

    nc = bacc.Bacc("TRN2", target_bir_lowering=False, num_devices=1)
    arrays, tensors = {}, {}
    for name, a in _layout(inputs).items():
        a = np.ascontiguousarray(a)
        arrays[f"in_{name}"] = a
        tensors[name] = nc.dram_tensor(f"in_{name}", a.shape, mybir.dt.from_np(a.dtype), kind="ExternalInput").ap()
    tensors["out"] = nc.dram_tensor("out_x", (B * S, D), F32, kind="ExternalOutput").ap()
    build(nc, tensors)
    r = run_bass_kernel_spmd(nc, [arrays], core_ids=[0])
    return r.results[0]["out_x"].reshape(B, S, D)
```

```python
from contextlib import ExitStack

import concourse.bass as bass
from concourse import mybir

F32 = mybir.dt.float32
F32R = mybir.dt.float32r
BF16 = mybir.dt.bfloat16
U32 = mybir.dt.uint32
ALU = mybir.AluOpType
ACT = mybir.ActivationFunctionType
AX = mybir.AxisListType

P = 128
B, S, D = 8, 512, 256
NT = S // P
DC = D // P
TT = B * NT
H0, HD = 4, 64
F0 = 1024
H1 = 16
NE, FE = 8, 512
FC = FE // P
EPS_LN = 1e-5
EPS_HEAD = 1e-6
EPS_Q = 1e-5
QB = 127.0
ROUND = 12582912.0
LOWEST = -3.0e38
HUGE = 1.0e30


class Steps:

    def __init__(self, eng, sem, per=0):
        self.eng, self.sem, self.per, self.base, self.n = eng, sem, per, 0, 0

    def begin(self, it):
        self.base, self.n = it * self.per, 0

    def __call__(self, ins):
        ins.then_inc(self.sem, 1)
        self.n += 1
        self.eng.wait_ge(self.sem, self.base + self.n)

    def end(self):
        assert self.n == self.per, (self.n, self.per)


def stand_alone(eng, k):
    eng.sem_inc(k.passed, 1)


class Core:

    def __init__(self, nc, ctx):
        self.nc = nc
        self.passed = ctx.enter_context(nc.semaphore("waits_passed"))

        def sb(name, shape, dt=F32):
            return ctx.enter_context(nc.sbuf_tensor(name, shape, dt))

        self.x = sb("x_res", [P, TT, D])
        self.ctxT = sb("ctxT", [P, DC, B * S])
        self.xnT = sb("xnT", [P, DC, B * S])
        self.ident = sb("ident", [P, P])
        self.identb = sb("identb", [P, P], BF16)
        self.tg = sb("tanh_gates", [P, 4])
        self.neg_half = sb("neg_half", [P, 32])


def phase_scope(nc, tag):
    ctx = ExitStack()

    def sb(name, shape, dt=F32):
        return ctx.enter_context(nc.sbuf_tensor(f"{tag}_{name}", shape, dt))

    def ps(name, shape, dt=F32):
        return ctx.enter_context(nc.psum_tensor(f"{tag}_{name}", shape, dt))

    def sem(name):
        return ctx.enter_context(nc.semaphore(f"{tag}_{name}"))

    return ctx, sb, ps, sem


def load_phase(nc, k, d):
    ctx, sb, ps, sem = phase_scope(nc, "ld")
    with ctx:
        raw = sb("raw_gates", [P, 4])
        loaded, gates_in, blank, made = sem("loaded"), sem("gates_in"), sem("blank"), sem("made")
        with nc.Block() as block:
            @block.sync
            def _(sp):
                sp.dma_start(k.x[:], d["x"].rearrange("(t p) d -> p t d", p=P)).then_inc(loaded, 16)
                sp.dma_start(k.ctxT[:], d["ctxT"].rearrange("(c p) n -> p c n", p=P)).then_inc(loaded, 16)
                sp.wait_ge(loaded, 32)

            @block.scalar
            def _(act):
                for n, (g, at) in enumerate((("g_xattn", 0), ("g_ffn", 0), ("g_xattn", 1), ("g_ffn", 1))):
                    src = d[g][at:at + 1].rearrange("(a b) -> a b", a=1).broadcast_to([P, 1])
                    act.dma_start(raw[:, n:n + 1], src).then_inc(gates_in, 16)
                act.wait_ge(gates_in, 64)
                act.activation(k.tg[:], raw[:], ACT.Tanh).then_inc(made, 1)

            @block.gpsimd
            def _(pool):
                pool.memset(k.ident[:], 0.0).then_inc(blank, 1)
                pool.memset(k.identb[:], 0.0).then_inc(blank, 1)
                pool.memset(k.neg_half[:], -0.5).then_inc(blank, 1)
                pool.wait_ge(blank, 3)
                for m in (k.ident, k.identb):
                    pool.affine_select(out=m[:], in_=m[:], compare_op=ALU.not_equal, fill=1.0, base=0,
                                       pattern=[[-1, P]], channel_multiplier=1).then_inc(made, 1)


def norm_phase(nc, k, tag, rows=None, loads=None):
    ctx, sb, ps, sem = phase_scope(nc, tag)
    with ctx:
        stats = sb("stats", [P, 2, NT, 6])
        mv = sb("mean_var", [P, 2, NT, 2])
        veps = sb("var_eps", [P, 2, NT])
        rstd = sb("rstd", [P, 2, NT])
        xn = sb("xn", [P, 2, NT, D])
        tp = [ps(f"turned{i}", [P, S]) for i in range(2 * DC)]
        v_step, rstd_ready, xn_ready = sem("v_step"), sem("rstd_ready"), sem("xn_ready")
        turned, copied = sem("turned"), sem("copied")
        with nc.Block() as block:
            if loads is not None:
                @block.sync
                def _(sp):
                    loads(sp)

            @block.vector
            def _(dve):
                step = Steps(dve, v_step, 3)
                with dve.Fori(0, B // 2) as i:
                    for u in range(2):
                        b = 2 * i + u
                        step.begin(b)
                        for t in range(NT):
                            last = dve.bn_stats(stats[:, u, t, :], k.x[:, bass.ds(NT * b + t, 1), :])
                        step(last)
                        stand_alone(dve, k)
                        for t in range(NT):
                            last = dve.bn_aggr(mv[:, u, t, :], stats[:, u, t, :])
                        step(last)
                        step(dve.tensor_scalar(veps[:, u, :], mv[:, u, :, 1], EPS_LN, None, ALU.add))
                        step.end()
                        dve.wait_ge(rstd_ready, b + 1)
                        dve.wait_ge(turned, b + 1)
                        if rows is not None:
                            dve.wait_ge(copied, b + 1)
                        for t in range(NT):
                            last = dve.tensor_scalar(xn[:, u, t, :], k.x[:, bass.ds(NT * b + t, 1), :],
                                                     mv[:, u, t, 0:1], rstd[:, u, t:t + 1],
                                                     ALU.subtract, ALU.mult)
                        last.then_inc(xn_ready, 1)

            @block.gpsimd
            def _(pool):
                with pool.Fori(0, B // 2) as i:
                    for u in range(2):
                        b = 2 * i + u
                        pool.wait_ge(v_step, 3 * b + 3)
                        pool.tensor_tensor(rstd[:, u, :], veps[:, u, :], k.neg_half[:, 0:NT],
                                           ALU.pow).then_inc(rstd_ready, 1)

            @block.scalar
            def _(act):
                act.sem_inc(copied, 2)
                with act.Fori(0, B // 2) as i:
                    for u in range(2):
                        b = 2 * i + u
                        act.wait_ge(turned, b + 3)
                        if rows is not None:
                            act.activation(rows[:, bass.ds(NT * b, NT), :], xn[:, u, :, :], ACT.Copy)
                        for c in range(DC):
                            last = act.activation(k.xnT[:, c, bass.ds(S * b, S)], tp[2 * u + c][:], ACT.Copy)
                        last.then_inc(copied, 1)

            @block.tensor
            def _(pe):
                pe.sem_inc(turned, 2)
                with pe.Fori(0, B // 2) as i:
                    for u in range(2):
                        b = 2 * i + u
                        pe.wait_ge(xn_ready, b + 1)
                        pe.wait_ge(copied, b + 1)
                        for c in range(DC):
                            for t in range(NT):
                                last = pe.transpose(tp[2 * u + c][:, t * P:(t + 1) * P],
                                                    xn[:, u, t, c * P:(c + 1) * P], k.ident[:])
                        last.then_inc(turned, 1)


GP = P + B - 1


def mlstm_phase(nc, k, d):
    ctx, sb, ps, sem = phase_scope(nc, "ml")
    R = 32 * H0
    with ctx:
        acol = sb("a_cols", [P, NT, H0, 32])
        exp_nmax = sb("exp_negmax_cols", [P, NT, H0, 32])
        m_rows = sb("M_rows", [P, B, S])
        scale_row = sb("scale_row", [P, D])
        with ExitStack() as gctx:
            _gates(nc, k, d, gctx, acol, exp_nmax, m_rows, scale_row)

        kz = sb("k_padded", [P, 2, DC, 2, S])
        va = sb("v_and_ones", [P, 2, NT, H0, HD + 1])
        mr = sb("M_rows_of_batch", [P, 2, S])
        mb = sb("M_all_partitions", [P, 2, S])
        md = sb("M_diagonal", [P, 2, NT, P])
        dt = sb("D_T", [P, 2, NT, S])
        oT = sb("o_T", [HD + 1, H0, S])
        o = sb("o", [P, 2, NT, H0, HD + 1])
        sq = sb("squares", [P, NT * H0, HD])
        st = sb("head_stats", [P, 8, NT * H0])
        y = sb("y", [P, 2, NT, D])
        qk = [ps(f"qk{j}", [P, S]) for j in range(NT)]
        op = ps("o_psum", [P, S])
        tp = [ps(f"o_turned{i}", [P, NT, HD + 1]) for i in range(2)]

        m_in = [sem("m_in0"), sem("m_in1")]
        zeroed, kv_in = sem("zeroed"), [sem("kv_in0"), sem("kv_in1")]
        qk_ready = sem("qk_ready")
        c_done = sem("c_done")
        cv_done = sem("cv_done")
        mb_ready = sem("mb_ready")
        d_exp = sem("d_exp")
        masked = sem("masked")
        ot_ready = sem("ot_ready")
        t_done = sem("t_done")
        o_ready = sem("o_ready")
        v_step, sq_ready, rs_ready = sem("v_step"), sem("sq_ready"), sem("rs_ready")
        y_ready = sem("y_ready")
        x_added = sem("x_added")
        p_step = sem("p_step")
        vsteps = 12
        with nc.Block() as block:
            @block.sync
            def _(sp):
                sp.wait_ge(zeroed, 2)
                with sp.Fori(0, B // 2) as i:
                    for u in range(2):
                        b = 2 * i + u
                        sp.wait_ge(cv_done, H0 * b + H0)
                        sp.wait_ge(mb_ready, H0 * b + H0)
                        for c in range(DC):
                            for half in range(2):
                                r = HD * half
                                sp.dma_start(kz[r:r + HD, u, c, half, :],
                                             d["ctxT"][c * P + r:c * P + r + HD, bass.ds(S * b, S)]).then_inc(kv_in[u], 16)
                        for h in range(H0):
                            r = 32 * h
                            sp.dma_start(mr[r:r + 1, u, :], m_rows[r:r + 1, bass.ds(b, 1), :].rearrange("p a s -> p (a s)")).then_inc(m_in[u], 16)
                        for j in range(NT):
                            src = d["ctx"][bass.ds(S * b + P * j, P), :].rearrange("p (h e) -> p h e", h=H0)
                            sp.dma_start(va[:, u, j, :, 0:HD], src).then_inc(kv_in[u], 16)

            @block.tensor
            def _(pe):
                pe.sem_inc(cv_done, 2 * H0)
                with pe.Fori(0, B // 2) as i:
                    for u in range(2):
                        b = 2 * i + u
                        pe.wait_ge(kv_in[u], 16 * 8 * (i + 1))

                        def turn(h):
                            n = H0 * b + h
                            pe.wait_ge(ot_ready, n + 2)
                            pe.wait_ge(o_ready, n + 1)
                            for j in range(NT):
                                last = pe.transpose(tp[h % 2][:, j, :], oT[:, h, j * P:(j + 1) * P],
                                                    k.ident[0:HD + 1, 0:HD + 1])
                            last.then_inc(t_done, 1)

                        for h in range(H0):
                            n = H0 * b + h
                            for j in range(NT):
                                w = S - P * j
                                pe.matmul(qk[j][:, 0:w], kz[:, u, h // 2, h % 2, j * P:(j + 1) * P],
                                          k.xnT[:, h // 2, bass.ds(S * b + P * j, w)],
                                          start=True, stop=True).then_inc(qk_ready, 1)
                            if h > 0:
                                turn(h - 1)
                            pe.wait_ge(ot_ready, n + 1)
                            for j in range(NT):
                                w = S - P * j
                                pe.wait_ge(c_done, NT * n + j + 1)
                                last = pe.matmul(op[0:HD + 1, j * P:S], va[:, u, j, h, :],
                                                 dt[:, h % 2, j, 0:w], start=(j == 0), stop=(j == NT - 1))
                            last.then_inc(cv_done, 1)
                        turn(H0 - 1)

            @block.gpsimd
            def _(pool):
                pool.sem_inc(x_added, 2)
                pool.sem_inc(masked, 1)
                pool.sem_inc(mb_ready, 2 * H0)
                huge = pool.to_reg(HUGE)
                pool.memset(kz[:], 0.0).then_inc(zeroed, 1)
                pool.memset(va[:, :, :, :, HD:HD + 1], 1.0).then_inc(zeroed, 1)
                step = Steps(pool, p_step, 1)
                with pool.Fori(0, B // 2) as i:
                    for u in range(2):
                        b = 2 * i + u
                        for h in range(H0):
                            n = H0 * b + h
                            pool.wait_ge(d_exp, n + 1)
                            pool.wait_ge(masked, n + 1)
                            pool.wait_ge(m_in[u], 16 * H0 * (i + 1))
                            stand_alone(pool, k)
                            pool.partition_broadcast(mb[:, h % 2, :], mr[32 * h:32 * h + 1, u, :], P).then_inc(mb_ready, 1)
                            pool.wait_ge(mb_ready, 2 * H0 + n + 1)
                            stand_alone(pool, k)
                            pool.affine_select(out=md[:, h % 2, :, :],
                                               in_=mb[:, h % 2, :].rearrange("p (j s) -> p j s", j=NT),
                                               compare_op=ALU.is_ge, fill=huge, base=0,
                                               pattern=[[0, NT], [1, P]], channel_multiplier=-1).then_inc(masked, 1)
                        step.begin(b)
                        pool.wait_ge(v_step, vsteps * b + 11)
                        pool.tensor_tensor(st[:, 6, :], st[:, 4, :], k.neg_half[:, 0:NT * H0], ALU.pow).then_inc(rs_ready, 1)
                        pool.wait_ge(y_ready, b + 3)
                        row = scale_row[:].unsqueeze(1).broadcast_to([P, NT, D])
                        step(pool.tensor_tensor(y[:, u, :, :], y[:, u, :, :], row, ALU.mult))
                        stand_alone(pool, k)
                        xs = k.x[:, bass.ds(NT * b, NT), :]
                        pool.tensor_tensor(xs, xs, y[:, u, :, :], ALU.add).then_inc(x_added, 1)
                        step.end()
                        pool.wait_ge(x_added, b + 3)

            @block.scalar
            def _(act):
                act.sem_inc(ot_ready, 1)
                act.sem_inc(o_ready, 2)
                act.sem_inc(d_exp, 2)
                with act.Fori(0, B // 2) as i:
                    for u in range(2):
                        b = 2 * i + u

                        def decay(h):
                            n = H0 * b + h
                            act.wait_ge(masked, n + 2)
                            act.wait_ge(cv_done, 2 * H0 + n - 1)
                            for j in range(NT):
                                at = acol[:, j, h, bass.ds(b, 1)]
                                last = act.activation(dt[:, h % 2, j, 0:P], md[:, h % 2, j, :], ACT.Exp,
                                                      bias=at, scale=-1.0)
                                if j + 1 < NT:
                                    act.activation(dt[:, h % 2, j, P:S - P * j], mb[:, h % 2, P * (j + 1):S], ACT.Exp,
                                                   bias=at, scale=-1.0)
                            last.then_inc(d_exp, 1)

                        def out_copies(h):
                            n = H0 * b + h
                            act.wait_ge(cv_done, 2 * H0 + n + 1)
                            act.activation(oT[:, h, :], op[0:HD + 1, :], ACT.Copy).then_inc(ot_ready, 1)
                            act.wait_ge(t_done, n + 1)
                            if h == 0:
                                act.wait_ge(y_ready, b + 1)
                            act.activation(o[:, u, :, h, :], tp[h % 2][:], ACT.Copy).then_inc(o_ready, 1)

                        decay(0)
                        decay(1)
                        for h in range(H0):
                            out_copies(h)
                            if h + 2 < H0:
                                decay(h + 2)
                        act.wait_ge(v_step, vsteps * b + 7)
                        act.activation(sq[:], o[:, u, :, :, 0:HD].rearrange("p j h e -> p (j h) e"),
                                       ACT.Square).then_inc(sq_ready, 1)

            @block.vector
            def _(dve):
                dve.sem_inc(y_ready, 2)
                step = Steps(dve, v_step, vsteps)
                with dve.Fori(0, B // 2) as i:
                    for u in range(2):
                        b = 2 * i + u
                        for h in range(H0):
                            n = H0 * b + h
                            dve.wait_ge(d_exp, n + 3)
                            for j in range(NT):
                                w = S - P * j
                                dve.wait_ge(qk_ready, NT * n + j + 1)
                                dve.scalar_tensor_tensor(out=dt[:, h % 2, j, 0:w], in0=qk[j][:, 0:w], scalar=HD ** -0.5,
                                                         in1=dt[:, h % 2, j, 0:w], op0=ALU.mult,
                                                         op1=ALU.mult).then_inc(c_done, 1)
                        step.begin(b)
                        dve.wait_ge(o_ready, 2 + H0 * b + H0)
                        ov = o[:, u, :, :, 0:HD].rearrange("p j h e -> p (j h) e")
                        rows = lambda n: st[:, n, :]
                        wide = lambda n: st[:, n, :].unsqueeze(2).broadcast_to([P, NT * H0, HD])
                        sums = o[:, u, :, :, HD].rearrange("p j h -> p (j h)")
                        step(dve.scalar_tensor_tensor(out=rows(0), in0=sums, scalar=-1.0, in1=sums,
                                                      op0=ALU.mult, op1=ALU.max))
                        step(dve.scalar_tensor_tensor(out=rows(0), in0=rows(0), scalar=0.0,
                                                      in1=exp_nmax[:, :, :, bass.ds(b, 1)].rearrange("p j h e -> p (j h e)"),
                                                      op0=ALU.add, op1=ALU.max))
                        step(dve.tensor_scalar(rows(0), rows(0), EPS_HEAD, None, ALU.add))
                        step(dve.reciprocal(rows(1), rows(0)))
                        step(dve.tensor_reduce(rows(2), ov, AX.X, ALU.add))
                        step(dve.tensor_scalar(rows(2), rows(2), 1.0 / HD, None, ALU.mult))
                        step(dve.tensor_tensor(ov, ov, wide(2), ALU.subtract))
                        step(dve.tensor_tensor(rows(3), rows(1), rows(1), ALU.mult))
                        dve.wait_ge(sq_ready, b + 1)
                        step(dve.tensor_reduce(rows(4), sq[:], AX.X, ALU.add))
                        step(dve.tensor_tensor(rows(4), rows(4), rows(3), ALU.mult))
                        step(dve.tensor_scalar(rows(4), rows(4), 1.0 / HD, EPS_HEAD, ALU.mult, ALU.add))
                        dve.wait_ge(rs_ready, b + 1)
                        step(dve.tensor_tensor(rows(5), rows(1), rows(6), ALU.mult))
                        dve.wait_ge(x_added, b + 1)
                        dve.tensor_tensor(y[:, u, :, :].rearrange("p j (h e) -> p (j h) e", h=H0), ov, wide(5),
                                          ALU.mult).then_inc(y_ready, 1)
                        step.end()


def _gates(nc, k, d, ctx, acol, exp_nmax, m_rows, scale_row):
    def sb(name, shape, dt=F32):
        return ctx.enter_context(nc.sbuf_tensor(f"gate_{name}", shape, dt))

    def sem(name):
        return ctx.enter_context(nc.semaphore(f"gate_{name}"))

    gk = sb("kernels", [P, 3 * DC, GP])
    gkc = sb("context_kernels", [P, DC, GP])
    bias = sb("bias", [P, 1])
    g = sb("preact", [P, S])
    e = sb("e", [P, S])
    lf = sb("log_f", [P, S])
    lfi = sb("log_f_on_i_rows", [P, S])
    zero = sb("zero", [P, S])
    cs = sb("cumsum", [P, S])
    a = sb("a", [P, S])
    m = sb("M", [P, S])
    r = sb("neg_max", [P, S])
    scale_in = sb("scale_in", [P, D])
    gp = ctx.enter_context(nc.psum_tensor("gate_psum", [P, S], F32))
    ap_ = ctx.enter_context(nc.psum_tensor("gate_a_turned", [P, S], F32))
    rp = ctx.enter_context(nc.psum_tensor("gate_r_turned", [P, S], F32))
    kernels_in, bias_in, scale_loaded = sem("kernels_in"), sem("bias_in"), sem("scale_loaded")
    summed, v_step, a_step, blank = sem("summed"), sem("v_step"), sem("a_step"), sem("blank")
    gates_done, moved, spread, turned, cols = (sem("gates_done"), sem("moved"), sem("spread"),
                                               sem("turned"), sem("cols"))
    with nc.Block() as block:
        @block.sync
        def _(sp):
            sp.dma_start(gk[:], d["gate_kernels"].rearrange("(c p) n -> p c n", p=P)).then_inc(kernels_in, 16)
            sp.dma_start(bias[:], d["gate_bias"]).then_inc(bias_in, 16)
            sp.dma_start(scale_in[:], d["outnorm_scale"].rearrange("(a n) -> a n", a=1).broadcast_to([P, D])).then_inc(scale_loaded, 16)
            sp.wait_ge(v_step, 3)
            sp.wait_ge(blank, 2)
            for h in range(H0):
                sp.dma_start(lfi[32 * h:32 * h + B, :], lf[32 * h + B:32 * h + 2 * B, :]).then_inc(moved, 16)
            sp.wait_ge(v_step, 6)
            for h in range(H0):
                sp.dma_start(m_rows[32 * h:32 * h + 1, :, :], m[32 * h:32 * h + B, :]).then_inc(spread, 16)
            sp.wait_ge(spread, 16 * H0)

        @block.gpsimd
        def _(pool):
            pool.memset(lfi[:], 0.0).then_inc(blank, 1)
            pool.memset(zero[:], 0.0).then_inc(blank, 1)

        @block.tensor
        def _(pe):
            pe.wait_ge(summed, 1)
            for b in range(B):
                for n in range(2 * DC):
                    c = n % DC
                    w = gk[:, c, :] if n < DC else gkc[:, c, :]
                    mv = k.xnT if n < DC else k.ctxT
                    last = pe.matmul(gp[:], w[:, B - 1 - b:B - 1 - b + P], mv[:, c, b * S:(b + 1) * S],
                                     start=(b == 0 and n == 0), stop=(b == B - 1 and n == 2 * DC - 1))
            last.then_inc(gates_done, 1)
            pe.wait_ge(v_step, 7)
            for t in range(NT):
                pe.transpose(ap_[:, t * P:(t + 1) * P], a[:, t * P:(t + 1) * P], k.ident[:])
                last = pe.transpose(rp[:, t * P:(t + 1) * P], r[:, t * P:(t + 1) * P], k.ident[:])
            last.then_inc(turned, 1)

        @block.scalar
        def _(act):
            act.wait_ge(bias_in, 16)
            act.wait_ge(gates_done, 1)
            act.activation(g[:], gp[:], ACT.Identity, bias=bias[:]).then_inc(a_step, 1)
            act.wait_ge(v_step, 1)
            act.activation(e[:], e[:], ACT.Exp, scale=-1.0).then_inc(a_step, 1)
            act.wait_ge(v_step, 2)
            act.activation(e[:], e[:], ACT.Ln).then_inc(a_step, 1)
            act.wait_ge(turned, 1)
            act.activation(exp_nmax[:].rearrange("p j h e -> p (j h e)"), rp[:], ACT.Exp)

        @block.vector
        def _(dve):
            dve.wait_ge(kernels_in, 16)
            dve.tensor_tensor(gkc[:], gk[:, DC:2 * DC, :], gk[:, 2 * DC:3 * DC, :], ALU.add).then_inc(summed, 1)
            dve.wait_ge(scale_loaded, 16)
            dve.tensor_scalar(scale_row[:], scale_in[:], k.tg[:, 0:1], None, ALU.mult)
            step = Steps(dve, v_step)
            dve.wait_ge(a_step, 1)
            step(dve.scalar_tensor_tensor(out=e[:], in0=g[:], scalar=-1.0, in1=g[:], op0=ALU.mult, op1=ALU.max))
            dve.wait_ge(a_step, 2)
            step(dve.tensor_scalar(e[:], e[:], 1.0, None, ALU.add))
            dve.wait_ge(a_step, 3)
            step(dve.scalar_tensor_tensor(out=lf[:], in0=g[:], scalar=0.0, in1=e[:], op0=ALU.min, op1=ALU.subtract))
            dve.wait_ge(moved, 16 * H0)
            step(dve.tensor_tensor_scan(cs[:], lfi[:], zero[:], 0.0, ALU.add, ALU.add))
            step(dve.tensor_tensor(a[:], g[:], cs[:], ALU.subtract))
            step(dve.tensor_tensor_scan(m[:], a[:], a[:], LOWEST, ALU.max, ALU.max))
            step(dve.scalar_tensor_tensor(out=r[:], in0=cs[:], scalar=-1.0, in1=m[:], op0=ALU.mult, op1=ALU.subtract))
            dve.wait_ge(turned, 1)
            dve.tensor_copy(acol[:].rearrange("p j h e -> p (j h e)"), ap_[:])


def bitnet_phase(nc, k, d):
    ctx, sb, ps, sem = phase_scope(nc, "bn")
    with ctx:
        w1q = sb("w1q", [P, DC, F0], BF16)
        w2q = sb("w2q", [P, F0 // P, D], BF16)
        b1 = sb("b1_rows", [P, F0])
        b2 = sb("b2_rows", [P, NT, D])
        wcol = sb("weight_scale_cols", [P, 2])
        with ExitStack() as wctx:
            _ternary_weights(nc, k, d, wctx, w1q, w2q, b1, b2, wcol)

        KF = F0 // P
        NS = 9
        stats = sb("stats", [P, NT, 6])
        mv = sb("mean_var", [P, NT, 2])
        col = sb("token_cols", [P, NS, NT])
        xn = sb("xn", [P, NT, D])
        q = sb("q", [P, NT, D], BF16)
        qT = sb("qT", [P, DC, NT, P], BF16)
        h = sb("h", [P, NT, F0])
        hcol = sb("hidden_cols", [P, 4, NT])
        q2 = sb("q2", [P, 2, F0], BF16)
        hT = sb("hT", [P, 2, KF, P], BF16)
        round_col = sb("round_col", [P, 1])
        qTp = ps("qT_psum", [P, DC, NT, P], BF16)
        hp = [ps(f"h_psum{i}", [P, F0]) for i in range(2)]
        hTp = ps("hT_psum", [P, KF, P], BF16)
        op = [ps(f"out_psum{i}", [P, D]) for i in range(2)]

        vq, pq = sem("vector_q_steps"), sem("pool_q_steps")
        VQ, PQ = 8, 3
        turned1, qT_ready, mm1, h_ready, gelu = sem("turned1"), sem("qT_ready"), sem("mm1"), sem("h_ready"), sem("gelu")
        vb, scaled, q2_ready = sem("vector_b_steps"), sem("scaled"), sem("q2_ready")
        turned2, hT_ready, mm2, x_done = sem("turned2"), sem("hT_ready"), sem("mm2"), sem("x_done")
        normed = sem("normed")
        biased, const = sem("biased"), sem("const")
        LAST = B - 1

        def each_batch(eng, before, body, after):
            before()
            body(0, True, False)
            with eng.Fori(1, LAST) as i:
                body(i, False, False)
            body(LAST, False, True)
            after()

        with nc.Block() as block:
            @block.vector
            def _(dve):
                qstep = Steps(dve, vq, VQ)
                bstep = Steps(dve, vb, 4)

                def q_stats(b):
                    qstep.begin(b)
                    for t in range(NT):
                        last = dve.bn_stats(stats[:, t, :], k.x[:, bass.ds(NT * b + t, 1), :])
                    qstep(last)
                    stand_alone(dve, k)
                    for t in range(NT):
                        last = dve.bn_aggr(mv[:, t, :], stats[:, t, :])
                    qstep(last)
                    qstep(dve.tensor_scalar(col[:, 0, :], mv[:, :, 1], EPS_LN, None, ALU.add))

                def q_shift(b):
                    dve.wait_ge(pq, PQ * b + 1)
                    qstep(dve.scalar_tensor_tensor(out=col[:, 2, :], in0=mv[:, :, 0], scalar=-1.0, in1=col[:, 1, :],
                                                   op0=ALU.mult, op1=ALU.mult))

                def q_scale(b):
                    dve.wait_ge(normed, b + 1)
                    qstep(dve.tensor_reduce(col[:, 3, :], xn[:], AX.X, ALU.max, apply_absolute_value=True))
                    qstep(dve.tensor_scalar(col[:, 3, :], col[:, 3, :], EPS_Q, None, ALU.max))
                    qstep(dve.reciprocal(col[:, 4, :], col[:, 3, :]))
                    qstep(dve.tensor_scalar(col[:, 5, :], col[:, 4, :], QB, None, ALU.mult))
                    qstep.end()

                def scale_bias(b, t, first):
                    n = NT * b + t
                    if t == 0:
                        dve.tensor_scalar(col[:, 6, :], col[:, 3, :], wcol[:, 0:1], None, ALU.mult).then_inc(const, 1)
                        dve.wait_ge(const, b + 2)
                    if not first:
                        dve.wait_ge(q2_ready, n - 3)
                    dve.wait_ge(mm1, n + 1)
                    dve.scalar_tensor_tensor(out=h[:, t, :], in0=hp[t % 2][:], scalar=col[:, 6, t:t + 1], in1=b1[:],
                                             op0=ALU.mult, op1=ALU.add).then_inc(h_ready, 1)

                def hidden_scale(n, t):
                    bstep.begin(n)
                    dve.wait_ge(gelu, n + 1)
                    bstep(dve.tensor_reduce(hcol[:, 0, t:t + 1], h[:, t, :], AX.X, ALU.max, apply_absolute_value=True))
                    bstep(dve.tensor_scalar(hcol[:, 0, t:t + 1], hcol[:, 0, t:t + 1], EPS_Q, None, ALU.max))
                    bstep(dve.reciprocal(hcol[:, 1, t:t + 1], hcol[:, 0, t:t + 1]))
                    dve.tensor_scalar(hcol[:, 3, t:t + 1], hcol[:, 0, t:t + 1], wcol[:, 1:2], None, ALU.mult)
                    bstep(dve.tensor_scalar(hcol[:, 2, t:t + 1], hcol[:, 1, t:t + 1], QB, None, ALU.mult))
                    bstep.end()

                def add_out(b, n, t):
                    dve.wait_ge(biased, b + 1)
                    dve.wait_ge(mm2, n + 1)
                    xt = k.x[:, bass.ds(n, 1), :].rearrange("p a e -> p (a e)")
                    dve.scalar_tensor_tensor(out=xt, in0=op[t % 2][:], scalar=hcol[:, 3, t:t + 1], in1=xt,
                                             op0=ALU.mult, op1=ALU.add).then_inc(x_done, 1)

                def before():
                    dve.memset(round_col[:], ROUND).then_inc(const, 1)
                    q_stats(0)
                    q_shift(0)
                    q_scale(0)

                def body(b, first, last):
                    for t in range(NT):
                        n = NT * b + t
                        if not first:
                            add_out(b - 1, n - 4, t)
                        scale_bias(b, t, first)
                        if not (first and t == 0):
                            hidden_scale(n - 1, (t - 1) % NT)
                        if not last:
                            if t == 0:
                                q_stats(b + 1)
                            if t == 1:
                                q_shift(b + 1)
                            if t == 2:
                                dve.wait_ge(mm1, n + 1)
                                q_scale(b + 1)

                def after():
                    hidden_scale(TT - 1, NT - 1)
                    for t in range(NT):
                        add_out(LAST, NT * LAST + t, t)

                each_batch(dve, before, body, after)

            @block.gpsimd
            def _(pool):
                pstep = Steps(pool, pq, PQ)

                def q_rstd(b):
                    pstep.begin(b)
                    pool.wait_ge(vq, VQ * b + 3)
                    pstep(pool.tensor_tensor(col[:, 1, :], col[:, 0, :], k.neg_half[:, 0:NT], ALU.pow))

                def add_bias(b):
                    pool.wait_ge(normed, b + 1)
                    stand_alone(pool, k)
                    xs = k.x[:, bass.ds(NT * b, NT), :]
                    pool.tensor_tensor(xs, xs, b2[:], ALU.add).then_inc(biased, 1)

                def q_round(b, first):
                    pool.wait_ge(vq, VQ * b + 8)
                    stand_alone(pool, k)
                    for t in range(NT):
                        last = pool.tensor_scalar(xn[:, t, :], xn[:, t, :], col[:, 5, t:t + 1], ROUND, ALU.mult, ALU.add)
                    pstep(last)
                    if not first:
                        pool.wait_ge(turned1, b)
                    stand_alone(pool, k)
                    pstep(pool.tensor_scalar(q[:], xn[:], -ROUND, 1.0, ALU.add, ALU.mult))
                    pstep.end()

                def hidden_round(n, t, early):
                    pool.wait_ge(scaled, n + 1)
                    if not early:
                        pool.wait_ge(turned2, n - 1)
                    stand_alone(pool, k)
                    pool.tensor_scalar(q2[:, t % 2, :], h[:, t, :], -ROUND, 1.0, ALU.add, ALU.mult).then_inc(q2_ready, 1)

                def before():
                    q_rstd(0)
                    add_bias(0)
                    q_round(0, True)

                def body(b, first, last):
                    for t in range(NT):
                        n = NT * b + t
                        if not (first and t == 0):
                            hidden_round(n - 1, (t - 1) % NT, first and t < 3)
                        if not last:
                            if t == 0:
                                q_rstd(b + 1)
                            if t == 1:
                                add_bias(b + 1)
                            if t == 2:
                                q_round(b + 1, False)

                def after():
                    hidden_round(TT - 1, NT - 1, False)

                each_batch(pool, before, body, after)

            @block.tensor
            def _(pe):
                def first_product(b, t, first):
                    n = NT * b + t
                    if t == 0:
                        pe.wait_ge(pq, PQ * b + 3)
                        for c in range(DC):
                            for j in range(NT):
                                last = pe.transpose(qTp[:, c, j, :], q[:, j, c * P:(c + 1) * P], k.identb[:])
                        last.then_inc(turned1, 1)
                        pe.wait_ge(qT_ready, b + 1)
                    if not (first and t < 2):
                        pe.wait_ge(h_ready, n - 1)
                    for m in range(F0 // S):
                        for c in range(DC):
                            last = pe.matmul(hp[t % 2][:, m * S:(m + 1) * S], qT[:, c, t, :],
                                             w1q[:, c, m * S:(m + 1) * S], start=(c == 0), stop=(c == DC - 1))
                    last.then_inc(mm1, 1)

                def turn(n, t, early):
                    pe.wait_ge(q2_ready, n + 1)
                    if not early:
                        pe.wait_ge(hT_ready, n)
                    for c in range(KF):
                        last = pe.transpose(hTp[:, c, :], q2[:, t % 2, c * P:(c + 1) * P], k.identb[:])
                    last.then_inc(turned2, 1)

                def second_product(n, t, early):
                    pe.wait_ge(hT_ready, n + 1)
                    if not early:
                        pe.wait_ge(x_done, n - 1)
                    for c in range(KF):
                        last = pe.matmul(op[t % 2][:], hT[:, t % 2, c, :], w2q[:, c, :],
                                         start=(c == 0), stop=(c == KF - 1))
                    last.then_inc(mm2, 1)

                def body(b, first, last):
                    for t in range(NT):
                        n = NT * b + t
                        first_product(b, t, first)
                        if not (first and t < 3):
                            second_product(n - 3, (t - 3) % NT, first)
                        if not (first and t < 2):
                            turn(n - 2, (t - 2) % NT, first and t == 2)

                def after():
                    second_product(TT - 3, NT - 3, False)
                    turn(TT - 2, NT - 2, False)
                    second_product(TT - 2, NT - 2, False)
                    turn(TT - 1, NT - 1, False)
                    second_product(TT - 1, NT - 1, False)

                each_batch(pe, lambda: None, body, after)

            @block.scalar
            def _(act):
                def copy_qT(b):
                    act.wait_ge(turned1, b + 1)
                    act.activation(qT[:], qTp[:], ACT.Copy).then_inc(qT_ready, 1)

                def normalize(b):
                    act.wait_ge(vq, VQ * b + 4)
                    for t in range(NT):
                        last = act.activation(xn[:, t, :], k.x[:, bass.ds(NT * b + t, 1), :].rearrange("p a e -> p (a e)"),
                                              ACT.Identity, bias=col[:, 2, t:t + 1], scale=col[:, 1, t:t + 1])
                    last.then_inc(normed, 1)

                def do_gelu(n, t):
                    act.wait_ge(h_ready, n + 1)
                    act.activation(h[:, t, :], h[:, t, :], ACT.Gelu).then_inc(gelu, 1)

                def do_scale(n, t):
                    act.wait_ge(vb, 4 * n + 4)
                    act.activation(h[:, t, :], h[:, t, :], ACT.Identity, scale=hcol[:, 2, t:t + 1],
                                   bias=round_col[:]).then_inc(scaled, 1)

                def copy_hT(n, t, early):
                    act.wait_ge(turned2, n + 1)
                    if not early:
                        act.wait_ge(mm2, n - 1)
                    act.activation(hT[:, t % 2, :, :], hTp[:], ACT.Copy).then_inc(hT_ready, 1)

                def body(b, first, last):
                    for t in range(NT):
                        n = NT * b + t
                        if t == 0:
                            copy_qT(b)
                        do_gelu(n, t)
                        if not (first and t == 0):
                            do_scale(n - 1, (t - 1) % NT)
                        if not (first and t < 2):
                            copy_hT(n - 2, (t - 2) % NT, first)
                        if not last and t == 1:
                            act.wait_ge(turned1, b + 1)
                            normalize(b + 1)

                def after():
                    do_scale(TT - 1, NT - 1)
                    copy_hT(TT - 2, NT - 2, False)
                    copy_hT(TT - 1, NT - 1, False)

                each_batch(act, lambda: normalize(0), body, after)


def _ternary_weights(nc, k, d, ctx, w1q, w2q, b1, b2, wcol):
    def sb(name, shape, dt=F32):
        return ctx.enter_context(nc.sbuf_tensor(f"tw_{name}", shape, dt))

    def sem(name):
        return ctx.enter_context(nc.semaphore(f"tw_{name}"))

    N = F0 * D
    w = [sb("w1", [P, N // P]), sb("w2", [P, N // P])]
    part = sb("abs_sums", [P, 2])
    ones = sb("ones", [P, P])
    ws = sb("scales", [P, 2])
    inv = sb("inverse_scales", [P, 2])
    b2_in = sb("b2_in", [P, D])
    total = ctx.enter_context(nc.psum_tensor("tw_total", [P, 2], F32))
    w_in, b_in, v_step, totals = [sem("w1_in"), sem("w2_in")], sem("b_in"), sem("v_step"), sem("totals")
    with nc.Block() as block:
        @block.sync
        def _(sp):
            sp.dma_start(w[0][:].rearrange("p (c f) -> p c f", c=DC),
                         d["W1T"].rearrange("(c p) f -> p c f", p=P)).then_inc(w_in[0], 16)
            sp.dma_start(w[1][:].rearrange("p (c f) -> p c f", c=F0 // P),
                         d["W2T"].rearrange("(c p) f -> p c f", p=P)).then_inc(w_in[1], 16)
            sp.dma_start(b1[:], d["b1"].rearrange("(a n) -> a n", a=1).broadcast_to([P, F0])).then_inc(b_in, 16)
            sp.dma_start(b2_in[:], d["b2"].rearrange("(a n) -> a n", a=1).broadcast_to([P, D])).then_inc(b_in, 16)
            sp.wait_ge(b_in, 32)

        @block.tensor
        def _(pe):
            pe.wait_ge(v_step, 3)
            pe.matmul(total[:], ones[:], part[:], start=True, stop=True).then_inc(totals, 1)

        @block.vector
        def _(dve):
            step = Steps(dve, v_step)
            step(dve.memset(ones[:], 1.0))
            for n in range(2):
                dve.wait_ge(w_in[n], 16)
                step(dve.tensor_reduce(part[:, n:n + 1], w[n][:], AX.X, ALU.add, apply_absolute_value=True))
            dve.wait_ge(totals, 1)
            step(dve.tensor_scalar(ws[:], total[:], 1.0 / N, EPS_Q, ALU.mult, ALU.max))
            step(dve.reciprocal(inv[:], ws[:]))
            dve.tensor_scalar(wcol[:, 0:1], ws[:, 0:1], 1.0 / QB, None, ALU.mult)
            dve.tensor_scalar(wcol[:, 1:2], ws[:, 1:2], 1.0 / QB, k.tg[:, 1:2], ALU.mult, ALU.mult)
            for n in range(2):
                step(dve.tensor_scalar(w[n][:], w[n][:], inv[:, n:n + 1], ROUND, ALU.mult, ALU.add))
                step(dve.tensor_scalar(w[n][:], w[n][:], ROUND, 1.0, ALU.subtract, ALU.min))
                out = (w1q, w2q)[n][:].rearrange("p c f -> p (c f)")
                step(dve.tensor_scalar(out, w[n][:], -1.0, None, ALU.max))
            dve.wait_ge(b_in, 32)
            for t in range(NT):
                dve.tensor_scalar(b2[:, t, :], b2_in[:], k.tg[:, 1:2], None, ALU.mult)


def attention_phase(nc, k, d):
    ctx, sb, ps, sem = phase_scope(nc, "at")
    PAIRS = H1 // 2
    NSTEP = B * PAIRS
    TI = 2 * NT
    with ctx:
        wqkv = sb("w_qkv", [P, 2, DC, 3 * P])
        w0 = sb("w_0", [P, 2, D])
        qs = sb("q_stack", [P, 2, 2, S], F32R)
        kh = sb("k_hi_twice", [P, 2, 2, S], F32R)
        kl = sb("k_lo_twice", [P, 2, 2, S], F32R)
        vT = sb("v_T", [P, S])
        v = sb("v", [P, 2, NT, P])
        pr = sb("probs", [P, 4, S])
        pT = sb("probs_T", [P, 2, 2, NT, S])
        oT = sb("o_T", [P, S])
        nmax = sb("neg_max", [P, TI])
        sums = sb("sums", [P, TI])
        rinv = sb("inverse_sums", [P, TI])
        jp = [ps(f"proj{i}", [P, S]) for i in range(2)]
        sp_ = [ps(f"scores{i}", [P, S]) for i in range(2)]
        tp = [ps(f"turned{i}", [P, NT, P]) for i in range(2)]
        op = ps("out", [P, S])
        wp = ps("w0_out", [P, S])

        wqkv_in, w0_in = [sem("wqkv_in0"), sem("wqkv_in1")], [sem("w0_in0"), sem("w0_in1")]
        q_psum, k_psum, v_psum, vt_psum = sem("q_psum"), sem("k_psum"), sem("v_psum"), sem("vt_psum")
        q_hi, q_lo, k_hi, k_lo = sem("q_hi"), sem("q_lo"), sem("k_hi"), sem("k_lo")
        k_twice = [sem("k_twice0"), sem("k_twice1")]
        vT_sb, v_sb = sem("vT_sb"), sem("v_sb")
        scored, maxed, exped, inverted = sem("scored"), sem("maxed"), sem("exped"), sem("inverted")
        normed, turned, even_copied, odd_copied = sem("normed"), sem("turned"), sem("even_copied"), sem("odd_copied")
        av, o_copied, w0_done, x_added = sem("av"), sem("o_copied"), sem("w0_done"), sem("x_added")

        def steps(eng, before, body, after):
            before()
            body(0, 0, True, False)
            with eng.Fori(0, (NSTEP - 2) // 2) as i:
                body(2 * i + 1, 1, False, False)
                body(2 * i + 2, 0, False, False)
            body(NSTEP - 1, 1, False, True)
            after()

        HALVES = (slice(0, HD), slice(HD, P))

        with nc.Block() as block:
            @block.sync
            def _(sp):
                def load_qkv(s, u):
                    src = d["w_qkv"][bass.ds(s % PAIRS, 1), :, :].rearrange("a (c p) n -> p (a c) n", p=P)
                    sp.dma_start(wqkv[:, u, :, :], src).then_inc(wqkv_in[u], 16)

                def load_w0(s, u):
                    src = d["w_0"][bass.ds(s % PAIRS, 1), :, :].rearrange("a p n -> (a p) n")
                    sp.dma_start(w0[:, u, :], src).then_inc(w0_in[u], 16)

                def k_again(s, u):
                    sp.wait_ge(k_hi, s + 1)
                    for hd in range(2):
                        sp.dma_start(kh[HALVES[1 - hd], u, hd, :].bitcast(F32),
                                     kh[HALVES[hd], u, hd, :].bitcast(F32)).then_inc(k_twice[u], 16)
                    sp.wait_ge(k_lo, s + 1)
                    for hd in range(2):
                        sp.dma_start(kl[HALVES[1 - hd], u, hd, :].bitcast(F32),
                                     kl[HALVES[hd], u, hd, :].bitcast(F32)).then_inc(k_twice[u], 16)

                def before():
                    for n in range(2):
                        load_qkv(n, n)
                        load_w0(n, n)
                    k_again(0, 0)
                    sp.wait_ge(v_psum, 1)
                    load_qkv(2, 0)

                def body(s, u, first, last):
                    if last:
                        return
                    k_again(s + 1, 1 - u)
                    sp.wait_ge(v_psum, s + 2)
                    load_qkv(s + 3, 1 - u)
                    if not first:
                        sp.wait_ge(w0_done, s)
                        load_w0(s + 1, 1 - u)

                steps(sp, before, body, lambda: (sp.wait_ge(wqkv_in[0], 16 * (NSTEP // 2 + 1)),
                                                 sp.wait_ge(wqkv_in[1], 16 * (NSTEP // 2 + 1))))

            @block.tensor
            def _(pe):
                def project(s, u, part, bank, done):
                    at = bass.ds(S * (s // PAIRS), S)
                    src = k.xnT if part == 0 else k.ctxT
                    for c in range(DC):
                        last = pe.matmul(jp[bank][:], wqkv[:, u, c, part * P:(part + 1) * P], src[:, c, at],
                                         start=(c == 0), stop=(c == DC - 1))
                    last.then_inc(done, 1)

                def project_q(s, u, early):
                    pe.wait_ge(wqkv_in[u], 16 * (s // 2 + 1))
                    if not early:
                        pe.wait_ge(vT_sb, s)
                    project(s, u, 0, 0, q_psum)

                def project_k(s, u, early):
                    if not early:
                        pe.wait_ge(v_sb, s)
                    project(s, u, 1, 1, k_psum)

                def project_v(s, u):
                    pe.wait_ge(q_hi, s + 1)
                    pe.wait_ge(q_lo, s + 1)
                    project(s, u, 2, 0, v_psum)

                def turn_v(s):
                    pe.wait_ge(k_hi, s + 1)
                    pe.wait_ge(k_lo, s + 1)
                    pe.wait_ge(vT_sb, s + 1)
                    for j in range(NT):
                        last = pe.transpose(jp[1][:, j * P:(j + 1) * P], vT[:, j * P:(j + 1) * P], k.ident[:])
                    last.then_inc(vt_psum, 1)

                def scores(s, u, i, first):
                    hd, m = i // NT, i % NT
                    if i == 0:
                        pe.wait_ge(q_hi, s + 1)
                        pe.wait_ge(q_lo, s + 1)
                        pe.wait_ge(k_twice[u], 64 * (s // 2 + 1))
                    if not (first and i < 2):
                        pe.wait_ge(exped, TI * s + i - 1)
                    lhs = qs[:, u, hd, m * P:(m + 1) * P]
                    pe.matmul(sp_[i % 2][:], lhs, kh[:, u, hd, :], start=True, stop=False)
                    pe.matmul(sp_[i % 2][:], lhs, kl[:, u, hd, :], start=False, stop=True).then_inc(scored, 1)

                def turn(s, i, first):
                    pe.wait_ge(normed, TI * s + i + 1)
                    if not (first and i < 2):
                        pe.wait_ge((even_copied, odd_copied)[i % 2], NT * s + i // 2)
                    for j in range(NT):
                        last = pe.transpose(tp[i % 2][:, j, :], pr[:, i % 4, j * P:(j + 1) * P], k.ident[:])
                    last.then_inc(turned, 1)

                def weigh_v(s, u):
                    pe.wait_ge(even_copied, NT * (s + 1))
                    pe.wait_ge(odd_copied, NT * (s + 1))
                    pe.wait_ge(v_sb, s + 1)
                    pe.wait_ge(x_added, s + 1)
                    for j in range(NT):
                        for hd in range(2):
                            last = pe.matmul(op[HALVES[hd], :], v[:, u, j, HALVES[hd]], pT[:, u, hd, j, :],
                                             start=(j == 0), stop=(j == NT - 1))
                    last.then_inc(av, 1)

                def output(s, u):
                    pe.wait_ge(o_copied, s + 1)
                    pe.wait_ge(w0_in[u], 16 * (s // 2 + 1))
                    for m in range(NT):
                        bank = (wp, op)[m // 2]
                        last = pe.matmul(bank[:, (m % 2) * D:(m % 2 + 1) * D], oT[:, m * P:(m + 1) * P], w0[:, u, :],
                                         start=True, stop=True)
                    last.then_inc(w0_done, 1)

                def before():
                    project_q(0, 0, True)
                    project_k(0, 0, True)
                    project_v(0, 0)
                    turn_v(0)

                def body(s, u, first, last):
                    for i in range(TI):
                        scores(s, u, i, first)
                        if i >= 3:
                            turn(s, i - 3, first)
                        elif not first:
                            turn(s - 1, i - 3 + TI, False)
                        if not last:
                            if i == 0:
                                project_q(s + 1, 1 - u, False)
                            if i == 2:
                                project_k(s + 1, 1 - u, False)
                            if i == 5:
                                project_v(s + 1, 1 - u)
                            if i == 7:
                                turn_v(s + 1)
                        if not first:
                            if i == 4:
                                weigh_v(s - 1, 1 - u)
                            if i == 6:
                                output(s - 1, 1 - u)

                def after():
                    for i in range(TI - 3, TI):
                        turn(NSTEP - 1, i, False)
                    weigh_v(NSTEP - 1, 1)
                    output(NSTEP - 1, 1)

                steps(pe, before, body, after)

            @block.scalar
            def _(act):
                def hi(s, u, psum_ready, bank, dst, done, scale):
                    act.wait_ge(psum_ready, s + 1)
                    for hd in range(2):
                        last = act.activation(dst[HALVES[hd], u, hd, :], jp[bank][HALVES[hd], :], ACT.Copy, scale=scale)
                    last.then_inc(done, 1)

                def exponent(s, i, first):
                    act.wait_ge(maxed, TI * s + i + 1)
                    if not (first and i < 4):
                        act.wait_ge(turned, TI * s + i - 3)
                    act.activation(pr[:, i % 4, :], sp_[i % 2][:], ACT.Exp, bias=nmax[:, i:i + 1],
                                   accum_out=sums[:, i:i + 1]).then_inc(exped, 1)

                def copy_turned(s, u, i):
                    act.wait_ge(turned, TI * s + i + 1)
                    m = i % NT
                    act.activation(pT[:, u, i // NT, :, m * P:(m + 1) * P], tp[i % 2][:], ACT.Copy).then_inc(even_copied, 1)

                def copy_vT(s):
                    act.wait_ge(v_psum, s + 1)
                    act.activation(vT[:], jp[0][:], ACT.Copy).then_inc(vT_sb, 1)

                def copy_o(s):
                    act.wait_ge(av, s + 1)
                    act.activation(oT[:], op[:], ACT.Copy).then_inc(o_copied, 1)

                def before():
                    hi(0, 0, q_psum, 0, qs, q_hi, HD ** -0.5)
                    hi(0, 0, k_psum, 1, kh, k_hi, 1.0)
                    copy_vT(0)

                def body(s, u, first, last):
                    for i in range(TI):
                        exponent(s, i, first)
                        if i % 2:
                            if i >= 3:
                                copy_turned(s, u, i - 3)
                            elif not first:
                                copy_turned(s - 1, 1 - u, i - 3 + TI)
                        if not last:
                            if i == 0:
                                hi(s + 1, 1 - u, q_psum, 0, qs, q_hi, HD ** -0.5)
                            if i == 2:
                                hi(s + 1, 1 - u, k_psum, 1, kh, k_hi, 1.0)
                            if i == 6:
                                copy_vT(s + 1)
                        if not first and i == 5:
                            copy_o(s - 1)

                def after():
                    copy_turned(NSTEP - 1, 1, TI - 2)
                    copy_o(NSTEP - 1)

                steps(act, before, body, after)

            @block.vector
            def _(dve):
                def lo(s, u, psum_ready, hi_ready, bank, his, dst, flip, done, scale):
                    dve.wait_ge(hi_ready, s + 1)
                    for hd in range(2):
                        to = HALVES[1 - hd] if flip else HALVES[hd]
                        last = dve.scalar_tensor_tensor(out=dst[to, u, hd, :], in0=jp[bank][HALVES[hd], :], scalar=scale,
                                                        in1=his[HALVES[hd], u, hd, :].bitcast(F32),
                                                        op0=ALU.mult, op1=ALU.subtract)
                    last.then_inc(done, 1)

                def row_max(s, i):
                    dve.wait_ge(scored, TI * s + i + 1)
                    dve.tensor_reduce(nmax[:, i:i + 1], sp_[i % 2][:], AX.X, ALU.max, negate=True).then_inc(maxed, 1)

                def invert(s, i):
                    dve.wait_ge(exped, TI * s + i + 1)
                    dve.reciprocal(rinv[:, i:i + 1], sums[:, i:i + 1]).then_inc(inverted, 1)

                def copy_turned(s, u, i):
                    dve.wait_ge(turned, TI * s + i + 1)
                    m = i % NT
                    dve.tensor_copy(pT[:, u, i // NT, :, m * P:(m + 1) * P], tp[i % 2][:]).then_inc(odd_copied, 1)

                def copy_v(s, u, early):
                    dve.wait_ge(vt_psum, s + 1)
                    if not early:
                        dve.wait_ge(av, s - 1)
                    dve.tensor_copy(v[:, u, :, :].rearrange("p j e -> p (j e)"), jp[1][:]).then_inc(v_sb, 1)

                def add_out(s):
                    dve.wait_ge(w0_done, s + 1)
                    for m in range(2):
                        xs = k.x[:, bass.ds(NT * (s // PAIRS) + 2 * m, 2), :]
                        bank = (wp, op)[m][:].rearrange("p (t e) -> p t e", t=2)
                        last = dve.scalar_tensor_tensor(out=xs, in0=bank, scalar=k.tg[:, 2:3], in1=xs,
                                                        op0=ALU.mult, op1=ALU.add)
                    last.then_inc(x_added, 1)
                    dve.wait_ge(x_added, s + 2)

                def before():
                    dve.sem_inc(x_added, 1)
                    lo(0, 0, q_psum, q_hi, 0, qs, qs, True, q_lo, HD ** -0.5)
                    lo(0, 0, k_psum, k_hi, 1, kh, kl, False, k_lo, 1.0)
                    copy_v(0, 0, True)

                def body(s, u, first, last):
                    for i in range(TI):
                        row_max(s, i)
                        if i > 0:
                            invert(s, i - 1)
                        elif not first:
                            invert(s - 1, TI - 1)
                        if i % 2 == 0:
                            if i >= 4:
                                copy_turned(s, u, i - 3)
                            elif not first:
                                copy_turned(s - 1, 1 - u, i - 3 + TI)
                        if not last:
                            if i == 1:
                                lo(s + 1, 1 - u, q_psum, q_hi, 0, qs, qs, True, q_lo, HD ** -0.5)
                            if i == 3:
                                lo(s + 1, 1 - u, k_psum, k_hi, 1, kh, kl, False, k_lo, 1.0)
                        if not first and i == 7:
                            add_out(s - 1)
                        if not last and i == 7:
                            copy_v(s + 1, 1 - u, first)

                def after():
                    invert(NSTEP - 1, TI - 1)
                    copy_turned(NSTEP - 1, 1, TI - 3)
                    copy_turned(NSTEP - 1, 1, TI - 1)
                    add_out(NSTEP - 1)

                steps(dve, before, body, after)

            @block.gpsimd
            def _(pool):
                def divide(s, i):
                    pool.wait_ge(inverted, TI * s + i + 1)
                    stand_alone(pool, k)
                    pool.tensor_scalar(pr[:, i % 4, :], pr[:, i % 4, :], rinv[:, i:i + 1], 1.0,
                                       ALU.mult, ALU.mult).then_inc(normed, 1)

                def body(s, u, first, last):
                    for i in range(TI):
                        if i > 0:
                            divide(s, i - 1)
                        elif not first:
                            divide(s - 1, TI - 1)

                steps(pool, lambda: None, body, lambda: divide(NSTEP - 1, TI - 1))


CAP = B * S + P
NBLK = 2 * B * S // P + NE - 1


class Routes:

    def __init__(self, nc, ctx):
        def sb(name, shape, dt=F32):
            return ctx.enter_context(nc.sbuf_tensor(f"route_{name}", shape, dt))

        self.weight = sb("weight", [P, 2, TT])
        self.out_row = sb("out_row", [P, 2, TT], U32)
        self.block_expert = sb("block_expert", [P, NBLK + 1], U32)
        self.block_row = sb("block_row", [P, NBLK + 1], U32)
        self.w1 = sb("w1", [P, NE, DC, FE])
        self.w2 = sb("w2", [P, NE, FC, D])
        self.w_in = ctx.enter_context(nc.semaphore("expert_weights_in"))
        self.expert_in = nc.dram_tensor("expert_in", (NE * CAP, D), F32, kind="Internal").ap()
        self.expert_out = nc.dram_tensor("expert_out", (NBLK * P, D), F32, kind="Internal").ap()


def router_phase(nc, k, d, ro, rows):
    ctx, sb, ps, sem = phase_scope(nc, "ro")
    ET = NE * TT
    with ctx:
        gw = sb("gate_w", [P, DC, NE])
        lT = sb("logits_T", [NE, 2, S])
        lg = sb("logits", [P, TT, NE])
        top = sb("top", [P, TT, 8])
        idx = sb("index", [P, TT, 8], U32)
        idf = sb("index_f32", [P, TT, 2])
        ex = sb("exp_difference", [P, 2, TT])
        ids = sb("expert_ids", [P, NE])
        region = sb("region_rows", [P, NE])
        blocks = sb("block_ids", [P, NBLK + 1])
        tri = sb("earlier_partitions", [P, P], BF16)
        ones = sb("ones", [P, P], BF16)
        goes_on = sb("same_expert", [P, NE, TT])
        zero8 = sb("zero8", [P, NE])
        zrow = sb("zero_rows", [P, D])
        mask = sb("masks", [P, 2, NE, TT])
        both = sb("both_masks", [P, NE, TT], BF16)
        tot = sb("tile_counts", [P, NE, TT])
        cum = sb("cumulated", [P, NE, TT])
        rank = sb("rank", [P, NE, TT])
        tmp = sb("tmp", [P, 2, NE, TT])
        slot = sb("slot_f32", [P, 2, TT])
        in_row = sb("in_row", [P, 2, TT], U32)
        e8 = sb("per_expert", [P, 6, NE])
        pad = sb("pad_row", [P, NE], U32)
        bl = sb("per_block", [P, 3, NBLK + 1, NE])
        bs = sb("block_sums", [P, 2, NBLK + 1])
        lp = [ps(f"logits_psum{i}", [P, S]) for i in range(2)]
        tp = ps("turned", [P, TT, NE])
        rp = ps("rank_psum", [P, ET])
        cp = ps("count_psum", [P, ET])
        gw_in, logits, copied, turned, made, v_step, exd = (sem("gw_in"), sem("logits_done"), sem("copied"),
                                                            sem("turned"), sem("made"), sem("v_step"), sem("exp_done"))
        counted, scattered, padded, rows_ready, pads_ready = (sem("counted"), sem("scattered"), sem("padded"),
                                                              sem("rows_ready"), sem("pads_ready"))
        with nc.Block() as block:
            @block.sync
            def _(sp):
                sp.dma_start(gw[:], d["gate_w"].rearrange("(c p) e -> p c e", p=P)).then_inc(gw_in, 16)
                sp.wait_ge(made, 9)
                sp.wait_ge(pads_ready, 1)
                for e in range(NE):
                    at = sp.value_load(pad[0:1, e:e + 1], min_val=0, max_val=NE * CAP - P)
                    sp.dma_start(ro.expert_in[bass.ds(at, P), :], zrow[:]).then_inc(padded, 16)
                sp.wait_ge(padded, 16 * NE)

            @block.gpsimd
            def _(pool):
                f = dict(allow_small_or_imprecise_dtypes=True)
                pool.iota(ids[:], [[1, NE]], base=0, channel_multiplier=0, **f).then_inc(made, 1)
                pool.iota(region[:], [[CAP, NE]], base=0, channel_multiplier=0, **f).then_inc(made, 1)
                pool.iota(blocks[:], [[1, NBLK + 1]], base=0, channel_multiplier=0, **f).then_inc(made, 1)
                pool.memset(tri[:], 1.0).then_inc(made, 1)
                pool.memset(ones[:], 1.0).then_inc(made, 1)
                pool.memset(zero8[:], 0.0).then_inc(made, 1)
                pool.memset(goes_on[:], 1.0).then_inc(made, 1)
                pool.memset(zrow[:], 0.0).then_inc(made, 1)
                pool.wait_ge(made, 8)
                pool.memset(goes_on[:, :, 0:1], 0.0).then_inc(made, 1)
                pool.affine_select(out=tri[:], in_=tri[:], compare_op=ALU.is_gt, fill=0.0, base=0,
                                   pattern=[[1, P]], channel_multiplier=-1).then_inc(made, 1)
                pool.wait_ge(rows_ready, 1)
                for t in range(TT):
                    for n in range(2):
                        pool.indirect_dma_start(ro.expert_in, bass.IndirectOffsetOnAxis(ap=in_row[:, n, t:t + 1], axis=0),
                                                rows[:, t, :], None).then_inc(scattered, 16)
                pool.wait_ge(scattered, 16 * 2 * TT)

            def turn_logits(pe, b):
                pe.wait_ge(copied, b + 1)
                for t in range(NT):
                    last = pe.transpose(tp[:, NT * b + t, :], lT[:, b % 2, t * P:(t + 1) * P], k.ident[0:NE, 0:NE])
                last.then_inc(turned, 1)

            @block.tensor
            def _(pe):
                pe.wait_ge(gw_in, 16)
                for b in range(B):
                    if b >= 2:
                        pe.wait_ge(copied, b - 1)
                    for c in range(DC):
                        last = pe.matmul(lp[b % 2][0:NE, :], gw[:, c, :], k.xnT[:, c, b * S:(b + 1) * S],
                                         start=(c == 0), stop=(c == DC - 1))
                    last.then_inc(logits, 1)
                    if b > 0:
                        turn_logits(pe, b - 1)
                turn_logits(pe, B - 1)
                pe.wait_ge(made, 10)
                pe.wait_ge(v_step, 12)
                both_c = both[:].rearrange("p e t -> p (e t)")
                pe.matmul(rp[:], tri[:], both_c, start=True, stop=True)
                pe.matmul(cp[:], ones[:], both_c, start=True, stop=True).then_inc(counted, 1)

            @block.scalar
            def _(act):
                for b in range(B):
                    act.wait_ge(logits, b + 1)
                    if b >= 2:
                        act.wait_ge(turned, b - 1)
                    act.activation(lT[:, b % 2, :], lp[b % 2][0:NE, :], ACT.Copy).then_inc(copied, 1)
                act.wait_ge(v_step, 4)
                act.activation(ex[:, 0, :], ex[:, 0, :], ACT.Exp).then_inc(exd, 1)

            @block.vector
            def _(dve):
                step = Steps(dve, v_step)
                dve.wait_ge(turned, B)
                step(dve.tensor_copy(lg[:], tp[:]))
                for t in range(TT):
                    last = dve.max(top[:, t, :], lg[:, t, :])
                step(last)
                for t in range(TT):
                    last = dve.max_index(idx[:, t, :], top[:, t, :], lg[:, t, :])
                step(last)
                step(dve.tensor_tensor(ex[:, 0, :], top[:, :, 1], top[:, :, 0], ALU.subtract))
                step(dve.tensor_copy(idf[:], idx[:, :, 0:2]))
                dve.wait_ge(exd, 1)
                step(dve.tensor_scalar(ex[:, 1, :], ex[:, 0, :], 1.0, None, ALU.add))
                step(dve.reciprocal(ex[:, 1, :], ex[:, 1, :]))
                step(dve.tensor_scalar(ro.weight[:, 0, :], ex[:, 1, :], k.tg[:, 3:4], None, ALU.mult))
                step(dve.tensor_tensor(ro.weight[:, 1, :], ex[:, 0, :], ro.weight[:, 0, :], ALU.mult))
                dve.wait_ge(made, 10)
                ids_w = ids[:].unsqueeze(2).broadcast_to([P, NE, TT])
                for n in range(2):
                    step(dve.tensor_tensor(mask[:, n, :, :], ids_w, idf[:, :, n].unsqueeze(1).broadcast_to([P, NE, TT]),
                                           ALU.is_equal))
                step(dve.tensor_tensor(both[:], mask[:, 0, :, :], mask[:, 1, :, :], ALU.add))
                dve.wait_ge(counted, 1)
                flat = lambda x: x[:].rearrange("p e t -> p (e t)")
                step(dve.tensor_copy(flat(tot), cp[:]))
                step(dve.tensor_tensor_scan(flat(cum), flat(goes_on), flat(tot), 0.0, ALU.mult, ALU.add))
                n_e = cum[:, :, TT - 1]
                step(dve.tensor_tensor(e8[:, 4, :], region[:], n_e, ALU.add))
                dve.tensor_copy(pad[:], e8[:, 4, :]).then_inc(pads_ready, 1)
                step(dve.tensor_scalar(e8[:, 0, :], n_e, 1.0 / P, (P - 1.0) / P - 0.5 + 0.5 / P, ALU.mult, ALU.add))
                step(dve.tensor_scalar(e8[:, 0, :], e8[:, 0, :], ROUND, ROUND, ALU.add, ALU.subtract))
                step(dve.tensor_tensor_scan(e8[:, 1, :], e8[:, 0, :], zero8[:], 0.0, ALU.add, ALU.add))
                step(dve.tensor_tensor(e8[:, 2, :], e8[:, 1, :], e8[:, 0, :], ALU.subtract))
                step(dve.tensor_tensor(flat(rank), rp[:], flat(cum), ALU.add))
                step(dve.tensor_tensor(rank[:], rank[:], tot[:], ALU.subtract))
                step(dve.tensor_tensor(cum[:], rank[:], region[:].unsqueeze(2).broadcast_to([P, NE, TT]), ALU.add))
                for n in range(2):
                    last = dve.tensor_tensor(tmp[:, n, :, :], cum[:], mask[:, n, :, :], ALU.mult)
                step(last)
                for n in range(2):
                    last = dve.tensor_reduce(slot[:, n, :], tmp[:, n, :, :].rearrange("p e t -> p t e"), AX.X, ALU.add)
                step(last)
                step(dve.tensor_copy(in_row[:], slot[:]))
                dve.nop().then_inc(rows_ready, 1)
                step(dve.tensor_scalar(e8[:, 3, :], e8[:, 2, :], float(P), None, ALU.mult))
                step(dve.tensor_tensor(cum[:], rank[:], e8[:, 3, :].unsqueeze(2).broadcast_to([P, NE, TT]), ALU.add))
                for n in range(2):
                    last = dve.tensor_tensor(tmp[:, n, :, :], cum[:], mask[:, n, :, :], ALU.mult)
                step(last)
                for n in range(2):
                    last = dve.tensor_reduce(slot[:, n, :], tmp[:, n, :, :].rearrange("p e t -> p t e"), AX.X, ALU.add)
                step(last)
                step(dve.tensor_copy(ro.out_row[:], slot[:]))
                wide_e = lambda x: x.unsqueeze(1).broadcast_to([P, NBLK + 1, NE])
                wide_b = lambda x: x.unsqueeze(2).broadcast_to([P, NBLK + 1, NE])
                step(dve.tensor_tensor(bl[:, 0, :, :], wide_b(blocks[:]), wide_e(e8[:, 1, :]), ALU.is_ge))
                step(dve.tensor_tensor(bl[:, 1, :, :], wide_b(blocks[:]), wide_e(e8[:, 2, :]), ALU.is_ge))
                step(dve.tensor_tensor(bl[:, 1, :, :], bl[:, 1, :, :], bl[:, 0, :, :], ALU.subtract))
                step(dve.tensor_tensor(e8[:, 5, :], region[:], e8[:, 3, :], ALU.subtract))
                step(dve.tensor_scalar(blocks[:], blocks[:], float(P), None, ALU.mult))
                step(dve.tensor_tensor(bl[:, 2, :, :], wide_b(blocks[:]), wide_e(e8[:, 5, :]), ALU.add))
                step(dve.tensor_tensor(bl[:, 2, :, :], bl[:, 2, :, :], bl[:, 1, :, :], ALU.mult))
                step(dve.tensor_reduce(bs[:, 0, :], bl[:, 0, :, :], AX.X, ALU.add))
                step(dve.tensor_reduce(bs[:, 1, :], bl[:, 2, :, :], AX.X, ALU.add))
                step(dve.tensor_scalar(ro.block_expert[:], bs[:, 0, :], NE - 1.0, None, ALU.min))
                step(dve.tensor_copy(ro.block_row[:], bs[:, 1, :]))


def experts_phase(nc, k, d, ro):
    ctx, sb, ps, sem = phase_scope(nc, "ex")
    XB = 4
    with ctx:
        xr = sb("rows", [P, XB, D])
        xT = sb("rows_T", [P, 2, DC, P])
        h = sb("hidden", [P, 2, FE])
        hT = sb("hidden_T", [P, 2, FC, P])
        y = sb("y", [P, 2, D])
        tp = ps("rows_turned", [P, DC, P])
        hp = [ps(f"h_psum{i}", [P, FE]) for i in range(2)]
        hTp = ps("hidden_turned", [P, FC, P])
        yp = [ps(f"y_psum{i}", [P, D]) for i in range(2)]
        x_in = [sem(f"x_in{i}") for i in range(XB)]
        x_turned, xT_ready, h_done, silu = sem("x_turned"), sem("xT_ready"), sem("h_done"), sem("silu")
        h_turned, hT_ready, y_done, y_copied = sem("h_turned"), sem("hT_ready"), sem("y_done"), sem("y_copied")
        y_out = [sem("y_out0"), sem("y_out1")]
        L = NBLK - 1
        assert L % XB == 2

        def blocks(eng, body):
            body(0, 0, True, False)
            with eng.Fori(0, L // XB) as i:
                for u in range(1, XB + 1):
                    body(XB * i + u, u % XB, False, False)
            body(L - 1, 1, False, False)
            body(L, 2, False, True)

        with nc.Block() as block:
            @block.sync
            def _(sp):
                def load(j, m):
                    at = sp.value_load(ro.block_row[0:1, bass.ds(j, 1)], min_val=0, max_val=NE * CAP - P)
                    sp.dma_start(xr[:, m, :], ro.expert_in[bass.ds(at, P), :]).then_inc(x_in[m], 16)

                def body(j, m, first, last):
                    if first:
                        for n in range(XB):
                            load(n, n)
                        return
                    if not isinstance(j, int):
                        sp.wait_ge(x_turned, j)
                        load(j - 1 + XB, (m - 1) % XB)
                    store(j - 1, (m - 1) % 2)
                    if last:
                        store(j, m % 2)
                        sp.wait_ge(y_out[0], 16 * (L // 2 + 1))
                        sp.wait_ge(y_out[1], 16 * (L // 2))
                        sp.wait_ge(x_in[3], 16 * (L // XB + 1))

                def store(j, u):
                    sp.wait_ge(y_copied, j + 3)
                    sp.dma_start(ro.expert_out[bass.ds(P * j, P), :], y[:, u, :]).then_inc(y_out[u], 16)

                blocks(sp, body)

            @block.tensor
            def _(pe):
                def expert(j):
                    return pe.value_load(ro.block_expert[0:1, bass.ds(j, 1)], min_val=0, max_val=NE - 1)

                def turn_rows(j, m, early):
                    pe.wait_ge(x_in[m], 16 * (j // XB + 1))
                    if not early:
                        pe.wait_ge(xT_ready, j)
                    for c in range(DC):
                        last = pe.transpose(tp[:, c, :], xr[:, m, c * P:(c + 1) * P], k.ident[:])
                    last.then_inc(x_turned, 1)

                def first_product(j, u, early):
                    e = expert(j)
                    pe.wait_ge(xT_ready, j + 1)
                    if not early:
                        pe.wait_ge(silu, j - 1)
                    for c in range(DC):
                        last = pe.matmul(hp[u][:], xT[:, u, c, :], ro.w1[:, bass.ds(e, 1), c, :],
                                         start=(c == 0), stop=(c == DC - 1))
                    last.then_inc(h_done, 1)

                def turn_hidden(j, u):
                    pe.wait_ge(silu, j + 1)
                    pe.wait_ge(hT_ready, j + 1)
                    for f in range(FC):
                        last = pe.transpose(hTp[:, f, :], h[:, u, f * P:(f + 1) * P], k.ident[:])
                    last.then_inc(h_turned, 1)

                def second_product(j, u):
                    e = expert(j)
                    pe.wait_ge(hT_ready, j + 2)
                    pe.wait_ge(y_copied, j + 1)
                    for f in range(FC):
                        last = pe.matmul(yp[u][:], hT[:, u, f, :], ro.w2[:, bass.ds(e, 1), f, :],
                                         start=(f == 0), stop=(f == FC - 1))
                    last.then_inc(y_done, 1)

                def body(j, m, first, last):
                    u = m % 2
                    if first:
                        pe.wait_ge(ro.w_in, 32)
                        turn_rows(0, 0, True)
                    else:
                        turn_hidden(j - 1, 1 - u)
                    first_product(j, u, isinstance(j, int) and j < 2)
                    if not last:
                        turn_rows(j + 1, (m + 1) % XB, False)
                    if not first:
                        second_product(j - 1, 1 - u)
                    if last:
                        turn_hidden(j, u)
                        second_product(j, u)

                blocks(pe, body)

            @block.scalar
            def _(act):
                def copy_rows(j, u):
                    act.wait_ge(x_turned, j + 1)
                    act.activation(xT[:, u, :, :], tp[:], ACT.Copy).then_inc(xT_ready, 1)

                def body(j, m, first, last):
                    u = m % 2
                    if first:
                        copy_rows(0, 0)
                    act.wait_ge(h_done, j + 1)
                    act.activation(h[:, u, :], hp[u][:], ACT.Silu).then_inc(silu, 1)
                    if not last:
                        copy_rows(j + 1, 1 - u)

                blocks(act, body)

            @block.vector
            def _(dve):
                def copy_hidden(j, u):
                    dve.wait_ge(h_turned, j + 1)
                    dve.tensor_copy(hT[:, u, :, :], hTp[:]).then_inc(hT_ready, 1)

                def copy_y(j, u):
                    dve.wait_ge(y_done, j + 1)
                    dve.tensor_copy(y[:, u, :], yp[u][:]).then_inc(y_copied, 1)

                def body(j, m, first, last):
                    u = m % 2
                    if first:
                        dve.sem_inc(hT_ready, 1)
                        dve.sem_inc(y_copied, 2)
                    else:
                        copy_hidden(j - 1, 1 - u)
                        if not (isinstance(j, int) and j < 3):
                            dve.wait_ge(y_out[1 - u], 16 * ((j - 1) // 2))
                        copy_y(j - 1, 1 - u)
                    if last:
                        copy_hidden(j, u)
                        dve.wait_ge(y_out[u], 16 * (j // 2))
                        copy_y(j, u)

                blocks(dve, body)


def combine_phase(nc, k, d, ro):
    ctx, sb, ps, sem = phase_scope(nc, "co")
    RING = 8
    with ctx:
        g = sb("gathered", [P, RING, D])
        got = [sem(f"got{i}") for i in range(RING)]
        added, stored = sem("added"), sem("stored")
        out = d["out"].rearrange("(t p) d -> p t d", p=P)
        with nc.Block() as block:
            @block.gpsimd
            def _(pool):
                for n in range(2 * TT):
                    if n >= RING:
                        pool.wait_ge(added, n - RING + 1)
                    pool.indirect_dma_start(g[:, n % RING, :], None, ro.expert_out,
                                            bass.IndirectOffsetOnAxis(ap=ro.out_row[:, n % 2, n // 2:n // 2 + 1], axis=0)
                                            ).then_inc(got[n % RING], 16)

            @block.vector
            def _(dve):
                for n in range(2 * TT):
                    dve.wait_ge(got[n % RING], 16 * (n // RING + 1))
                    if n % 2:
                        dve.wait_ge(added, n)
                    t = n // 2
                    dve.scalar_tensor_tensor(out=k.x[:, t, :], in0=g[:, n % RING, :], scalar=ro.weight[:, n % 2, t:t + 1],
                                             in1=k.x[:, t, :], op0=ALU.mult, op1=ALU.add).then_inc(added, 1)

            @block.sync
            def _(sp):
                for b in range(B):
                    sp.wait_ge(added, 2 * NT * (b + 1))
                    sp.dma_start(out[:, NT * b:NT * (b + 1), :], k.x[:, NT * b:NT * (b + 1), :]).then_inc(stored, 16)
                sp.wait_ge(stored, 16 * B)


def store_phase(nc, k, d):
    ctx, sb, ps, sem = phase_scope(nc, "st")
    with ctx:
        stored = sem("stored")
        with nc.Block() as block:
            @block.sync
            def _(sp):
                sp.dma_start(d["out"].rearrange("(t p) d -> p t d", p=P), k.x[:]).then_inc(stored, 16)
                sp.wait_ge(stored, 16)


def build(nc, d, phases="abcd"):
    with ExitStack() as ctx:
        k = Core(nc, ctx)
        load_phase(nc, k, d)
        if "a" in phases:
            norm_phase(nc, k, "n0")
            mlstm_phase(nc, k, d)
        if "b" in phases:
            bitnet_phase(nc, k, d)
        if "c" in phases:
            norm_phase(nc, k, "n2")
            attention_phase(nc, k, d)
        if "d" in phases:
            ro = Routes(nc, ctx)
            rows = k.ctxT[:].rearrange("p c n -> p (c n)").rearrange("p (t e) -> p t e", t=TT)

            def expert_weights(sp):
                sp.dma_start(ro.w1[:], d["w1"].rearrange("e (c p) n -> p e c n", p=P)).then_inc(ro.w_in, 16)
                sp.dma_start(ro.w2[:], d["w2"].rearrange("e (c p) n -> p e c n", p=P)).then_inc(ro.w_in, 16)

            norm_phase(nc, k, "n3", rows, expert_weights)
            router_phase(nc, k, d, ro, rows)
            experts_phase(nc, k, d, ro)
            combine_phase(nc, k, d, ro)
        else:
            store_phase(nc, k, d)


def _layout(i):
    import numpy as np

    def flip(a):
        return np.ascontiguousarray(np.asarray(a).T)

    x = np.asarray(i["x"]).reshape(B * S, D)
    context = np.asarray(i["ctx_1024"]).reshape(B * S, D)
    gk = np.zeros((3 * D, GP), np.float32)
    gb = np.zeros((H0, 32), np.float32)
    for h in range(H0):
        gk[:, 32 * h + B - 1] = i["L0_xattn_igate_kernel"][:, h]
        gk[:, 32 * h + 2 * B - 1] = i["L0_xattn_fgate_kernel"][:, h]
        gb[h, 0:B] = i["L0_xattn_igate_bias"][h]
        gb[h, B:2 * B] = i["L0_xattn_fgate_bias"][h]
    wq = np.asarray(i["L1_xattn_Wq"]).reshape(HD, H1 // 2, 2, D)
    wkv = np.asarray(i["L1_xattn_Wkv"]).reshape(HD, 2, H1 // 2, 2, D)
    parts = [p.transpose(1, 3, 2, 0).reshape(H1 // 2, D, P) for p in (wq, wkv[:, 0], wkv[:, 1])]
    return {
        "x": x, "ctx": context, "ctxT": flip(context), "g_xattn": i["g_xattn"], "g_ffn": i["g_ffn"],
        "gate_kernels": gk, "gate_bias": gb.reshape(P, 1), "outnorm_scale": i["L0_xattn_outnorm_scale"],
        "W1T": flip(i["L0_ffn_W1"]), "W2T": flip(i["L0_ffn_W2"]), "b1": i["L0_ffn_b1"], "b2": i["L0_ffn_b2"],
        "w_qkv": np.concatenate(parts, axis=2), "w_0": flip(i["L1_xattn_W0"]).reshape(H1 // 2, P, D),
        "gate_w": i["L1_ffn_gate_w"], "w1": i["L1_ffn_w1"], "w2": i["L1_ffn_w2"],
    }


def kernel(**inputs):
    import numpy as np
    import concourse.bacc as bacc
    from concourse.bass_utils import run_bass_kernel_spmd

    nc = bacc.Bacc("TRN2", target_bir_lowering=False, num_devices=1)
    arrays, tensors = {}, {}
    for name, a in _layout(inputs).items():
        a = np.ascontiguousarray(a)
        arrays[f"in_{name}"] = a
        tensors[name] = nc.dram_tensor(f"in_{name}", a.shape, mybir.dt.from_np(a.dtype), kind="ExternalInput").ap()
    tensors["out"] = nc.dram_tensor("out_x", (B * S, D), F32, kind="ExternalOutput").ap()
    build(nc, tensors)
    r = run_bass_kernel_spmd(nc, [arrays], core_ids=[0])
    return r.results[0]["out_x"].reshape(B, S, D)
```
